# Optimizing a Trainium2 kernel written in Bass

```python
import numpy as np
import jax
import jax.numpy as jnp

def _softmax(x, axis=-1):
    return jax.nn.softmax(x, axis=axis)

def _gelu(x):
    return jax.nn.gelu(x, approximate=True)

def _silu(x):
    return jax.nn.silu(x)

def _sigmoid(x):
    return jax.nn.sigmoid(x)

def _layernorm(x, axis=-1, eps=1e-05):
    m = jnp.mean(x, axis=axis, keepdims=True)
    v = jnp.var(x, axis=axis, keepdims=True)
    return (x - m) / jnp.sqrt(v + eps)

def _scatter_add(tgt, idx, src, axis=0):
    return tgt.at[idx].add(src)

def _segment_sum(src, seg, n):
    return jax.ops.segment_sum(src, seg, n)
kernel_name = 'mk_xattn_ffn_d1_seqx_r2_44431e'

def setup_inputs(seed: int=0):
    np.random.seed(seed)
    _w = jnp.asarray

    def _rec_inputs():
        import jax
        import jax.numpy as jnp
        _rk = jax.random.key(seed)
        x = -0.0002928 + 1 * jax.random.normal(jax.random.fold_in(_rk, 1), (16, 256, 512), jnp.float32)
        _lenS = 256 - jax.random.randint(jax.random.fold_in(_rk, 7), (16,), 0, max(1, 256 // 4) + 1, jnp.int32)
        _lenS2 = 256 - jax.random.randint(jax.random.fold_in(_rk, 8), (16,), 0, max(1, 256 // 4) + 1, jnp.int32)
        _ctx_1024P = jax.random.normal(jax.random.fold_in(_rk, 11), (16, 16, 512), jnp.float32)
        _ctx_1024c = jax.random.dirichlet(jax.random.fold_in(_rk, 511), 0.3 * jnp.ones((16,), jnp.float32), (16, 256))
        _ctx_1024t = jnp.einsum('bsk,bkd->bsd', _ctx_1024c, _ctx_1024P)
        _ctx_1024t = _ctx_1024t * jax.lax.rsqrt(jnp.mean(jnp.square(_ctx_1024t)) + 1e-12) * 0.953939
        ctx_1024 = -1.39393e-06 + 0.999914 * (_ctx_1024t + 0.3 * jax.random.normal(jax.random.fold_in(_rk, 611), (16, 256, 512), jnp.float32))
        return (x, ctx_1024)
    x, ctx_1024 = _rec_inputs()

    def _L0_xattn_setup():
        import jax, jax.numpy as jnp
        import numpy as np
        B, S, H, NH = (2, 1024, 512, 4)
        DH = H // NH
        EPS_BACKEND = 1e-06
        EPS_LN = 1e-06

        def _mlstm_parallel_stabilized(q, k, v, igate_preact, fgate_preact):
            b, nh, s, dh = q.shape
            log_fg = jax.nn.log_sigmoid(fgate_preact)
            cs = jnp.concatenate([jnp.zeros((b, nh, 1), q.dtype), jnp.cumsum(log_fg[..., 0], axis=2)], axis=2)
            fg_matrix = cs[:, :, :, None] - cs[:, :, None, :]
            fg_matrix = fg_matrix[:, :, 1:, 1:]
            causal = jnp.tril(jnp.ones((s, s), dtype=bool))
            log_fg_matrix = jnp.where(causal, fg_matrix, -jnp.inf)
            log_D = log_fg_matrix + jnp.swapaxes(igate_preact, -2, -1)
            max_log_D = jnp.max(log_D, axis=-1, keepdims=True)
            D = jnp.exp(log_D - max_log_D)
            qk = jnp.einsum('bhsd,bhtd->bhst', q, k) / jnp.sqrt(jnp.asarray(dh, q.dtype))
            C = qk * D
            normalizer = jnp.maximum(jnp.abs(jnp.sum(C, axis=-1, keepdims=True)), jnp.exp(-max_log_D))
            C_norm = C / (normalizer + EPS_BACKEND)
            return jnp.einsum('bhst,bhtd->bhsd', C_norm, v)

        def _multihead_layernorm(x, scale):
            mean = jnp.mean(x, axis=-1, keepdims=True)
            var = jnp.var(x, axis=-1, keepdims=True)
            xn = (x - mean) * jax.lax.rsqrt(var + EPS_LN)
            return xn * scale.reshape(NH, 1, DH)
        key = jax.random.key(seed)
        kq, kk, kv, kib = jax.random.split(key, 4)
        q = jax.random.normal(kq, (B, S, H), dtype=jnp.float32)
        k = jax.random.normal(kk, (B, S, H), dtype=jnp.float32)
        v = jax.random.normal(kv, (B, S, H), dtype=jnp.float32)
        igate_kernel = jnp.zeros((3 * H, NH), dtype=jnp.float32)
        igate_bias = 0.1 * jax.random.normal(kib, (NH,), dtype=jnp.float32)
        fgate_kernel = jnp.zeros((3 * H, NH), dtype=jnp.float32)
        fgate_bias = jnp.linspace(3.0, 6.0, NH, dtype=jnp.float32)
        outnorm_scale = jnp.ones((H,), dtype=jnp.float32)
        return {'q': q, 'k': k, 'v': v, 'igate_kernel': igate_kernel, 'igate_bias': igate_bias, 'fgate_kernel': fgate_kernel, 'fgate_bias': fgate_bias, 'outnorm_scale': outnorm_scale}
    _L0_xattn_all = _L0_xattn_setup()
    _L0_xattn_in = {k: v for k, v in _L0_xattn_all.items() if k in ('igate_kernel', 'igate_bias', 'fgate_kernel', 'fgate_bias', 'outnorm_scale')}
    del _L0_xattn_all

    def _L0_ffn_setup():
        import jax, jax.numpy as jnp
        import numpy as np
        B, T, D, E, H = (4, 1024, 512, 4, 8)
        EPS = 1e-05

        def _uniform(k, shape, bound):
            return jax.random.uniform(k, shape, jnp.float32, -bound, bound)

        def _layernorm(x, w, b):
            mu = jnp.mean(x, axis=-1, keepdims=True)
            var = jnp.mean(jnp.square(x - mu), axis=-1, keepdims=True)
            return (x - mu) * jax.lax.rsqrt(var + EPS) * w + b
        key = jax.random.key(seed)
        ks = jax.random.split(key, 12)
        wb = np.sqrt(6.0 / D) / np.sqrt(6.0)
        wb = 1.0 / np.sqrt(D)
        return {'x': jax.random.normal(ks[0], (B, T, D), jnp.float32), 'router_prob': jax.random.uniform(ks[1], (B, T, E), jnp.float32), 'norm_w': jnp.ones((D,), jnp.float32), 'norm_b': jnp.zeros((D,), jnp.float32), 'q_w': _uniform(ks[2], (D, D), wb), 'q_b': _uniform(ks[3], (D,), wb), 'k_w': _uniform(ks[4], (D, D), wb), 'k_b': _uniform(ks[5], (D,), wb), 'v_w': _uniform(ks[6], (D, D), wb), 'v_b': _uniform(ks[7], (D,), wb), 'o_w': _uniform(ks[8], (D, D), wb), 'o_b': _uniform(ks[9], (D,), wb)}
    _L0_ffn_all = _L0_ffn_setup()
    _L0_ffn_in = {k: v for k, v in _L0_ffn_all.items() if k in ('router_prob', 'norm_w', 'norm_b', 'q_w', 'q_b', 'k_w', 'k_b', 'v_w', 'v_b', 'o_w', 'o_b')}
    del _L0_ffn_all
    return {'x': x, 'ctx_1024': ctx_1024, 'L0_xattn_igate_kernel': _L0_xattn_in['igate_kernel'], 'L0_xattn_igate_bias': _L0_xattn_in['igate_bias'], 'L0_xattn_fgate_kernel': _L0_xattn_in['fgate_kernel'], 'L0_xattn_fgate_bias': _L0_xattn_in['fgate_bias'], 'L0_xattn_outnorm_scale': _L0_xattn_in['outnorm_scale'], 'L0_ffn_router_prob': _L0_ffn_in['router_prob'], 'L0_ffn_norm_w': _L0_ffn_in['norm_w'], 'L0_ffn_norm_b': _L0_ffn_in['norm_b'], 'L0_ffn_q_w': _L0_ffn_in['q_w'], 'L0_ffn_q_b': _L0_ffn_in['q_b'], 'L0_ffn_k_w': _L0_ffn_in['k_w'], 'L0_ffn_k_b': _L0_ffn_in['k_b'], 'L0_ffn_v_w': _L0_ffn_in['v_w'], 'L0_ffn_v_b': _L0_ffn_in['v_b'], 'L0_ffn_o_w': _L0_ffn_in['o_w'], 'L0_ffn_o_b': _L0_ffn_in['o_b']}

def reference(x, ctx_1024, L0_xattn_igate_kernel, L0_xattn_igate_bias, L0_xattn_fgate_kernel, L0_xattn_fgate_bias, L0_xattn_outnorm_scale, L0_ffn_router_prob, L0_ffn_norm_w, L0_ffn_norm_b, L0_ffn_q_w, L0_ffn_q_b, L0_ffn_k_w, L0_ffn_k_b, L0_ffn_v_w, L0_ffn_v_b, L0_ffn_o_w, L0_ffn_o_b):
    import jax
    import jax.numpy as jnp

    def _L0_xattn_ref(q, k, v, igate_kernel, igate_bias, fgate_kernel, fgate_bias, outnorm_scale):
        import jax, jax.numpy as jnp
        import numpy as np
        B, S, H, NH = (2, 1024, 512, 4)
        DH = H // NH
        EPS_BACKEND = 1e-06
        EPS_LN = 1e-06

        def _mlstm_parallel_stabilized(q, k, v, igate_preact, fgate_preact):
            b, nh, s, dh = q.shape
            log_fg = jax.nn.log_sigmoid(fgate_preact)
            cs = jnp.concatenate([jnp.zeros((b, nh, 1), q.dtype), jnp.cumsum(log_fg[..., 0], axis=2)], axis=2)
            fg_matrix = cs[:, :, :, None] - cs[:, :, None, :]
            fg_matrix = fg_matrix[:, :, 1:, 1:]
            causal = jnp.tril(jnp.ones((s, s), dtype=bool))
            log_fg_matrix = jnp.where(causal, fg_matrix, -jnp.inf)
            log_D = log_fg_matrix + jnp.swapaxes(igate_preact, -2, -1)
            max_log_D = jnp.max(log_D, axis=-1, keepdims=True)
            D = jnp.exp(log_D - max_log_D)
            qk = jnp.einsum('bhsd,bhtd->bhst', q, k) / jnp.sqrt(jnp.asarray(dh, q.dtype))
            C = qk * D
            normalizer = jnp.maximum(jnp.abs(jnp.sum(C, axis=-1, keepdims=True)), jnp.exp(-max_log_D))
            C_norm = C / (normalizer + EPS_BACKEND)
            return jnp.einsum('bhst,bhtd->bhsd', C_norm, v)

        def _multihead_layernorm(x, scale):
            mean = jnp.mean(x, axis=-1, keepdims=True)
            var = jnp.var(x, axis=-1, keepdims=True)
            xn = (x - mean) * jax.lax.rsqrt(var + EPS_LN)
            return xn * scale.reshape(NH, 1, DH)
        b, s, h = q.shape
        gate_in = jnp.concatenate([q, k, v], axis=-1)
        ig = gate_in @ igate_kernel + igate_bias
        fg = gate_in @ fgate_kernel + fgate_bias
        ig = jnp.transpose(ig, (0, 2, 1))[..., None]
        fg = jnp.transpose(fg, (0, 2, 1))[..., None]
        qh = jnp.transpose(q.reshape(b, s, NH, DH), (0, 2, 1, 3))
        kh = jnp.transpose(k.reshape(b, s, NH, DH), (0, 2, 1, 3))
        vh = jnp.transpose(v.reshape(b, s, NH, DH), (0, 2, 1, 3))
        hs = _mlstm_parallel_stabilized(qh, kh, vh, ig, fg)
        hn = _multihead_layernorm(hs, outnorm_scale)
        return jnp.transpose(hn, (0, 2, 1, 3)).reshape(b, s, h)

    def _L0_ffn_ref(x, router_prob, norm_w, norm_b, q_w, q_b, k_w, k_b, v_w, v_b, o_w, o_b):
        import jax, jax.numpy as jnp
        import numpy as np
        B, T, D, E, H = (4, 1024, 512, 4, 8)
        EPS = 1e-05

        def _uniform(k, shape, bound):
            return jax.random.uniform(k, shape, jnp.float32, -bound, bound)

        def _layernorm(x, w, b):
            mu = jnp.mean(x, axis=-1, keepdims=True)
            var = jnp.mean(jnp.square(x - mu), axis=-1, keepdims=True)
            return (x - mu) * jax.lax.rsqrt(var + EPS) * w + b
        e_cnt = router_prob.shape[2]
        b, t, d = x.shape
        n = t // e_cnt
        h = H
        scale = d ** (-0.5)
        qs, ks_, vs = ([], [], [])
        for e in range(e_cnt):
            xe = x[:, e * n:(e + 1) * n, :]
            xn = _layernorm(xe, norm_w, norm_b)
            m = d // 2 ** e
            xm = xn[..., :m]
            qs.append(jnp.einsum('bnm,dm->bnd', xm, q_w[:, :m]) + q_b)
            ks_.append(jnp.einsum('bnm,dm->bnd', xm, k_w[:, :m]) + k_b)
            vs.append(jnp.einsum('bnm,dm->bnd', xm, v_w[:, :m]) + v_b)
        q = jnp.concatenate(qs, axis=1)
        k = jnp.concatenate(ks_, axis=1)
        v = jnp.concatenate(vs, axis=1)
        dh = d // h
        q = q.reshape(b, t, h, dh).transpose(0, 2, 1, 3)
        k = k.reshape(b, t, h, dh).transpose(0, 2, 1, 3)
        v = v.reshape(b, t, h, dh).transpose(0, 2, 1, 3)
        attn = jnp.einsum('bhqd,bhkd->bhqk', q, k) * scale
        attn = jax.nn.softmax(attn, axis=-1)
        attn_out = jnp.einsum('bhqk,bhkd->bhqd', attn, v)
        attn_out = attn_out.transpose(0, 2, 1, 3).reshape(b, t, d)
        outs = []
        for e in range(e_cnt):
            sl = slice(e * n, (e + 1) * n)
            m = d // 2 ** e
            xm = attn_out[:, sl, :m]
            out = jnp.einsum('bnm,om->bno', xm, o_w[:m, :m]) + o_b[:m]
            pad = d - m
            if pad:
                out = jnp.pad(out, ((0, 0), (0, 0), (0, pad)))
            outs.append(out + x[:, sl, :])
        return jnp.concatenate(outs, axis=1)
    x = x + _L0_xattn_ref(_layernorm(x, axis=-1), ctx_1024, ctx_1024, L0_xattn_igate_kernel, L0_xattn_igate_bias, L0_xattn_fgate_kernel, L0_xattn_fgate_bias, L0_xattn_outnorm_scale)
    x = x + _L0_ffn_ref(_layernorm(x, axis=-1), L0_ffn_router_prob, L0_ffn_norm_w, L0_ffn_norm_b, L0_ffn_q_w, L0_ffn_q_b, L0_ffn_k_w, L0_ffn_k_b, L0_ffn_v_w, L0_ffn_v_b, L0_ffn_o_w, L0_ffn_o_b)
    return x

_drawn_inputs = setup_inputs


def setup_inputs(seed=0):
    import zlib

    import numpy as np

    out = dict(_drawn_inputs(seed))
    spreads = {'L0_xattn_igate_kernel': (0.0, 0.1),
     'L0_xattn_fgate_kernel': (0.0, 0.1),
     'L0_xattn_outnorm_scale': (1.0, 0.2),
     'L0_ffn_norm_w': (1.0, 0.6),
     'L0_ffn_norm_b': (0.0, 0.8)}
    factors = {'L0_xattn_igate_bias': 8.0,
     'L0_ffn_q_w': 8.0,
     'L0_ffn_q_b': 8.0,
     'L0_ffn_k_w': 8.0,
     'L0_ffn_k_b': 64.0,
     'L0_ffn_v_w': 8.0,
     'L0_ffn_v_b': 8.0,
     'L0_ffn_o_w': 8.0,
     'L0_ffn_o_b': 58.589}
    for name, (base, spread) in spreads.items():
        noise = np.random.default_rng([zlib.crc32(name.encode()), seed]).standard_normal(out[name].shape)
        drawn = base * np.exp(spread * noise) if base else spread * noise
        out[name] = jnp.asarray(drawn.astype(out[name].dtype))
    for name, factor in factors.items():
        out[name] = (out[name] * factor).astype(out[name].dtype)
    return out
```

```python
from contextlib import ExitStack

import concourse.bass as bass
from concourse import mybir

F32 = mybir.dt.float32
ALU = mybir.AluOpType
ACT = mybir.ActivationFunctionType
AX = mybir.AxisListType

B, S, D = 16, 256, 512
P = 128
PB = 2
PAIRS = B // PB
T = S // P
C = D // P
NH, DH = 4, 128
E = 4
TE = S // E
FH = D // 8
EPS_X, EPS_GATE, EPS_HEAD, EPS_FFN = 1e-5, 1e-6, 1e-6, 1e-5
QK_SCALE = DH ** -0.5
ATT_SCALE = D ** -0.5
SPARE = 16
F_ROW = 32

BODY = [
    ("F", "nt", 0), ("F", "nt", 1), ("X", "xs", 0), ("X", "xs", 1), ("F", "k", 0), ("X", "xq", 0), ("X", "xq", 1),
    ("F", "k", 1), ("X", "xt", 0, 0), ("X", "xt", 0, 1), ("X", "xt", 1, 0), ("X", "xt", 1, 1), ("F", "k", 2),
    ("X", "gate"), ("F", "k", 3), ("X", "lsg"), ("F", "q0"), ("X", "scan"), ("F", "q1"), ("F", "x12", 0),
    ("F", "v", 0, 0), ("X", "cols"), ("X", "marg", 0, 0), ("F", "s", 0, 0), ("X", "marg", 0, 1), ("F", "s", 0, 1),
    ("X", "sx", 0, 0), ("F", "v", 0, 1), ("X", "sx", 0, 1), ("X", "u", 0, 0), ("F", "s", 0, 2), ("F", "pn", 0, 0),
    ("X", "sx", 0, 2), ("X", "u", 0, 1), ("F", "pn", 0, 1), ("X", "marg", 1, 0), ("X", "sx", 0, 3), ("F", "s", 0, 3),
    ("X", "u", 0, 2), ("F", "x12", 1), ("X", "sx", 1, 0), ("F", "v", 1, 0), ("X", "u", 0, 3), ("F", "pn", 0, 2),
    ("X", "sx", 1, 1), ("X", "tail_a", 0), ("F", "s", 1, 0), ("X", "u", 1, 0), ("X", "marg", 1, 1), ("F", "v", 1, 1),
    ("X", "sx", 1, 2), ("F", "pn", 0, 3), ("X", "u", 1, 1), ("F", "s", 1, 1), ("X", "sx", 1, 3), ("X", "tail_b", 0),
    ("F", "pt", 0, 0), ("X", "u", 1, 2), ("F", "s", 1, 2), ("X", "u", 1, 3), ("F", "pt", 0, 1), ("X", "tail_a", 1),
    ("F", "pn", 1, 0), ("F", "pt", 0, 2), ("F", "s", 1, 3), ("X", "tail_c", 0), ("F", "pt", 0, 3), ("F", "pn", 1, 1),
    ("F", "pv0", 0), ("X", "tail_b", 1), ("F", "pv1", 0), ("F", "pn", 1, 2), ("F", "pn", 1, 3), ("F", "pt", 1, 0),
    ("F", "pt", 1, 1), ("F", "o", 0, 0), ("F", "o", 0, 1), ("F", "pv0", 1), ("F", "pt", 1, 2), ("F", "pt", 1, 3),
    ("F", "pv1", 1), ("X", "tail_c", 1), ("F", "o", 1, 0), ("F", "o", 1, 1),
]
ORDER = {"first": [s for s in BODY if s[0] == "X"], "body": BODY, "last": [s for s in BODY if s[0] == "F"]}

RING_OF = {
    "nt": "turn", "xt": "turn", "pt": "turn",
    "k": "prod", "q0": "prod", "q1": "prod", "v": "prod", "pv0": "prod", "pv1": "prod", "o": "prod", "u": "prod",
    "s": "attn",
    "gate": "xatt", "cols": "xatt", "marg": "xatt", "sx": "xatt",
}
OWN = {"vector": {"X": 26, "F": 0}, "scalar": {"X": 2, "F": 0}, "gpsimd": {"X": 18, "F": 2}}


class Ring:

    def __init__(self, name, ctx, nc):
        self.banks = [ctx.enter_context(nc.psum_tensor(f"{name}{k}", [P, 512], F32)) for k in range(2)]
        self.filled = ctx.enter_context(nc.semaphore(f"{name}_filled"))
        self.jobs = {ph: [s for s in ORDER[ph] if RING_OF.get(s[1]) == name] for ph in ORDER}
        assert len(self.jobs["first"]) % 2 == 0 and len(self.jobs["body"]) % 2 == 0

    def place(self, phase, i, step):
        n, first, body = self.jobs[phase].index(step), len(self.jobs["first"]), len(self.jobs["body"])
        turn = {"first": 0, "body": i, "last": PAIRS - 1}[phase]
        return self.banks[n % 2], turn * body + (n if phase == "first" else n + first) + 1

    def before(self, phase, step):
        jobs = self.jobs[phase]
        n = jobs.index(step)
        if n >= 2:
            return [(jobs[n - 2], 0)]
        if phase == "first":
            return []
        turn = self.jobs["body"]
        f = [s for k, s in enumerate(turn) if s[0] == "F" and k % 2 == n][-1:]
        x = [s for s in turn if s[0] == "X"][-2:]
        return [(s, 1) for s in f + x]


def xattn_ffn(nc, x, ctx_in, ctx_t, ig_w, ig_b, fg_w, fg_b, on_scale, n_w, n_b,
              wq_t, q_b, wk_t, k_b, wv_t, v_b, wo_t, o_b, out):
    ctx = ExitStack()
    with ctx:
        def sb(name, shape):
            return ctx.enter_context(nc.sbuf_tensor(name, shape, F32))

        def sem(name):
            return ctx.enter_context(nc.semaphore(name))

        rings = {n: Ring(n, ctx, nc) for n in ("turn", "prod", "attn", "xatt")}

        ident = sb("ident", [P, P])
        neg_sel = sb("neg_sel", [NH, NH, P])
        wq, wk, wv, wo = (sb(n, [P, C, D]) for n in ("wq", "wk", "wv", "wo"))
        gate_raw = sb("gate_raw", [P, 2, 3 * C, NH])
        gate_w = sb("gate_w", [P, 2 * C, F_ROW + NH])
        gate_b = sb("gate_b", [F_ROW + NH, 1])
        on_row = sb("on_row", [P, D])
        o_bias = sb("o_bias", [P, T, D])
        qb, kb, vb, nw, nb = (sb(n, [P, C]) for n in ("qb", "kb", "vb", "nw", "nb"))
        qb_s = sb("qb_s", [P, C])
        pool_spare, dve_spare = sb("pool_spare", [1, SPARE + 1]), sb("dve_spare", [1, SPARE + 1])
        minus_half = sb("minus_half", [P, 8])
        ones_row = sb("ones_row", [NH, S])
        x_in = sb("x_in", [P, PB * T, D])
        x_res = sb("x_res", [P, PB * T, D])
        xn = sb("xn", [P, PB * T, D])
        xq = xn
        xq_t = sb("xq_t", [P, C, PB, S])
        kx_t = sb("kx_t", [P, PB * C, S])
        vx = sb("vx", [P, PB * T, NH, DH + 1])
        stat = sb("stat", [P, PB * T, 6])
        mv = sb("mv", [P, PB * T, 2])
        rstd = sb("rstd", [P, PB * T])
        ig = sb("ig", [NH, PB * S])
        fg = sb("fg", [NH, PB * S])
        ltmp = sb("ltmp", [NH, PB * S])
        cs = sb("cs", [NH, PB * S])
        g_rows = sb("g_rows", [P, PB * S])
        g_max = sb("g_max", [NH, PB * S])
        g_col = sb("g_col", [P, PB * T, NH])
        e_col = sb("e_col", [P, PB * T, NH])
        dec = sb("dec", [P, NH, 3, P])
        cmat = sb("cmat", [P, NH, 3, P])
        um = sb("um", [P, PB * T, NH, DH + 1])
        ustat = sb("ustat", [P, PB * T * NH, 6])
        umv = sb("umv", [P, PB * T * NH, 2])
        unorm = sb("unorm", [P, PB, T * NH])
        utmp = sb("utmp", [P, PB, T * NH])
        uvar = sb("uvar", [P, PB, T * NH])
        urstd = sb("urstd", [P, PB, T * NH])
        x1 = sb("x1", [P, PB * T, D])
        stat1 = sb("stat1", [P, PB * T, 6])
        mv1 = sb("mv1", [P, PB * T, 2])
        r1 = sb("r1", [P, PB * T])
        rp1 = sb("rp1", [P, PB * T])
        r2 = sb("r2", [P, PB * T])
        rtmp = sb("rtmp", [P, PB * T])
        n0 = sb("n0", [P, PB, S])
        n1 = sb("n1", [P, PB, 2 * TE])
        n2 = sb("n2", [P, 2, PB, TE])
        kt = sb("kt", [P, C, PB, S])
        q0 = sb("q0", [P, 2, PB, S])
        q1 = sb("q1", [P, 2, PB, 2 * TE])
        q23 = sb("q23", [P, 2, PB, 2, TE])
        vf = sb("vf", [P, PB * T, D])
        neg_max = sb("neg_max", [P, PB, 4, 2])
        p_sum = sb("p_sum", [P, PB, 4, 2])
        p_inv = sb("p_inv", [P, PB, 4, 2])
        prob = sb("prob", [P, PB, 4, 2, S])
        prob_t = sb("prob_t", [P, PB, T, 4, 2, P])
        a0 = sb("a0", [P, PB, S])
        a1 = sb("a1", [P, PB, 2 * TE])
        a23 = sb("a23", [P, PB, 2, TE])
        x12 = sb("x12", [P, PB * T, D])

        consts_in, weights_in = sem("consts_in"), sem("weights_in")
        ident_made = sem("ident_made")
        zeros_made = sem("zeros_made")
        consts_ready = sem("consts_ready")
        x_loaded, kx_loaded, vx_loaded, xres_loaded = (sem(n) for n in ("x_loaded", "kx_loaded", "vx_loaded", "xres_loaded"))
        stored = [sem(f"stored{b}") for b in range(PB)]
        x_var = sem("x_var")
        x_rstd = sem("x_rstd")
        xq_ready = sem("xq_ready")
        xqt_ready = sem("xqt_ready")
        fg_ready = sem("fg_ready")
        ln_ready = sem("ln_ready")
        rows_ready = sem("rows_ready")
        cols_ready = sem("cols_ready")
        arg_made = sem("arg_made")
        dec_made = sem("dec_made")
        dec_ready = sem("dec_ready")
        c_ready = sem("c_ready")
        u_ready = sem("u_ready")
        u_var = sem("u_var")
        u_rstd = sem("u_rstd")
        x1_ready = sem("x1_ready")
        x1_rstd = sem("x1_rstd")
        xn_ready = sem("xn_ready")
        n_ready = sem("n_ready")
        k_ready = sem("k_ready")
        q_ready = sem("q_ready")
        v_ready = sem("v_ready")
        max_ready = sem("max_ready")
        exp_done = sem("exp_done")
        inv_ready = sem("inv_ready")
        prob_ready = sem("prob_ready")
        probt_ready = sem("probt_ready")
        a_ready = sem("a_ready")
        x12_ready = sem("x12_ready")
        o_added = sem("o_added")
        own = {e: {s: sem(f"own_{e}_{s}") for s in "XF"} for e in OWN}

        READ = {
            "xt": lambda b, cc: (xqt_ready, 4, 2 * b + cc + 1), "nt": lambda k: (n_ready, 2, k + 1),
            "pt": lambda b, s: (probt_ready, 8, 4 * b + s + 1),
            "k": lambda c: (k_ready, 4, c + 1), "q0": lambda: (q_ready, 2, 1), "q1": lambda: (q_ready, 2, 2),
            "v": lambda b, t: (v_ready, 4, 2 * b + t + 1), "o": lambda b, t: (o_added, 4, 2 * b + t + 1),
            "pv0": lambda b: (a_ready, 4, 2 * b + 1), "pv1": lambda b: (a_ready, 4, 2 * b + 2),
            "u": lambda b, h: (u_ready, 8, 4 * b + h + 1), "s": lambda b, s: (exp_done, 8, 4 * b + s + 1),
            "gate": lambda: (fg_ready, 1, 1), "cols": lambda: (cols_ready, 1, 1),
            "marg": lambda b, k: (arg_made, 8, 4 * b + 2 * k + 2), "sx": lambda b, h: (c_ready, 8, 4 * b + h + 1),
        }

        def wait(eng, s, n):
            if not isinstance(n, int) or n > 0:
                eng.wait_ge(s, n)

        carried = [0]

        def carry(eng):
            carried[0] = k = carried[0] % SPARE + 1
            if eng.engine == nc.gpsimd.engine:
                eng.tensor_tensor(pool_spare[:, k:k + 1], pool_spare[:, 0:1], pool_spare[:, 0:1], ALU.mult)
            else:
                eng.tensor_copy(dve_spare[:, k:k + 1], dve_spare[:, 0:1])

        class Engine:

            def __init__(self, eng, name):
                self.eng, self.name = eng, name

            def link(self, ins, alone=False):
                s = own[self.name][self.stage]
                self.count[self.stage] += 1
                ins.then_inc(s, 1)
                self.eng.wait_ge(s, self.p * OWN[self.name][self.stage] + self.count[self.stage])
                if alone:
                    carry(self.eng)

            def run(self, steps, phase, i):
                self.count = {"X": 0, "F": 0}
                for step in ORDER[phase]:
                    self.stage, what, *args = step
                    self.p = {"first": 0, "body": i + (self.stage == "X"), "last": PAIRS - 1}[phase]
                    if what in RING_OF:
                        self.ring = rings[RING_OF[what]]
                        self.bank, self.fills = self.ring.place(phase, i, step)
                        self.before = self.ring.before(phase, step)
                        self.pair_of = {"X": i + 1 if phase == "body" else PAIRS if phase == "last" else 0,
                                        "F": i if phase == "body" else PAIRS - 1}
                    if what in steps:
                        steps[what](self.p, *args)
                for s in ("X", "F") if self.name in OWN else ():
                    if any(step[0] == s for step in ORDER[phase]):
                        assert self.count[s] == OWN[self.name][s], (self.name, s, self.count[s])

            def walk(self, steps):
                self.run(steps, "first", 0)
                self.run(steps, "body", 0)
                with self.eng.Fori(1, PAIRS - 1) as i:
                    self.run(steps, "body", i)
                self.run(steps, "last", 0)

            def bank_filled(self):
                self.eng.wait_ge(self.ring.filled, self.fills)

            def bank_free(self):
                for (stage, what, *args), back in self.before:
                    s, per_pair, n = READ[what](*args)
                    wait(self.eng, s, self.pair_of[stage] * per_pair + (0 if back else n))

        x_d = x.rearrange("(p b) (t q) d -> p q (b t) d", b=PB, q=P)
        ctx_d = ctx_in.rearrange("(p b) (t q) d -> p q (b t) d", b=PB, q=P)
        ctxt_d = ctx_t.rearrange("(p b) (c q) i -> p q (b c) i", b=PB, q=P)
        out_d = out.rearrange("p (t q) d -> p q t d", q=P)

        block = ctx.enter_context(nc.Block())

        @block.sync
        def _(sp):
            def load_x(p):
                sp.dma_start(x_in[:], x_d[p]).then_inc(x_loaded, 16)

            def load_kx(p):
                sp.dma_start(kx_t[:], ctxt_d[p]).then_inc(kx_loaded, 16)

            def load_vx(p):
                for g in range(PB * T):
                    sp.dma_start(vx[:, g, :, 0:DH], ctx_d[p, :, g, :].rearrange("q (h d) -> q h d", h=NH)).then_inc(vx_loaded, 16)

            def load_xres(p):
                sp.dma_start(x_res[:], x_d[p]).then_inc(xres_loaded, 16)

            def store(p, b):
                sp.wait_ge(o_added, 4 * p + 2 * b + 2)
                sp.dma_start(out_d[p * PB + b], x12[:, b * T:(b + 1) * T, :]).then_inc(stored[b], 16)

            load_x(0)
            sp.wait_ge(zeros_made, 1)
            for n, (tile, w) in enumerate(((gate_raw[:, 0], ig_w), (gate_raw[:, 1], fg_w))):
                sp.dma_start(tile, w.rearrange("(c p) h -> p c h", p=P)).then_inc(consts_in, 16)
            sp.dma_start(gate_b[0:NH], ig_b).then_inc(consts_in, 16)
            sp.dma_start(gate_b[F_ROW:F_ROW + NH], fg_b).then_inc(consts_in, 16)
            for tile, v in ((qb, q_b), (kb, k_b), (vb, v_b), (nw, n_w), (nb, n_b)):
                sp.dma_start(tile[:], v).then_inc(consts_in, 16)
            sp.dma_start(on_row[:], on_scale.partition_broadcast(P)).then_inc(consts_in, 16)
            for e in range(E):
                rows = slice(TE * (e % 2), TE * (e % 2 + 1))
                sp.dma_start(o_bias[rows, e // 2, 0:D >> e], o_b[:, 0:D >> e].partition_broadcast(TE)).then_inc(consts_in, 16)
            load_kx(0)
            load_vx(0)
            load_xres(0)
            for tile, w in ((wk, wk_t), (wq, wq_t), (wv, wv_t), (wo, wo_t)):
                sp.dma_start(tile[:], w.rearrange("(c p) n -> p c n", p=P)).then_inc(weights_in, 16)
            sp.wait_ge(xq_ready, 2)
            load_x(1)
            sp.wait_ge(c_ready, 8)
            load_kx(1)
            sp.wait_ge(u_ready, 8)
            load_vx(1)
            sp.wait_ge(x1_ready, 2)
            load_xres(1)
            with sp.Fori(0, PAIRS - 2) as i:
                sp.wait_ge(xq_ready, 2 * i + 4)
                load_x(i + 2)
                store(i, 0)
                sp.wait_ge(c_ready, 8 * i + 16)
                load_kx(i + 2)
                sp.wait_ge(u_ready, 8 * i + 16)
                load_vx(i + 2)
                sp.wait_ge(x1_ready, 2 * i + 4)
                load_xres(i + 2)
                store(i, 1)
            for p in (PAIRS - 2, PAIRS - 1):
                store(p, 0)
                store(p, 1)
            for b in range(PB):
                sp.wait_ge(stored[b], 16 * PAIRS)

        N_CONST = 16 * 14

        @block.gpsimd
        def _(pool):
            pool.memset(gate_b[:], 0.0)
            pool.memset(o_bias[:], 0.0).then_inc(zeros_made, 1)
            pool.memset(ident[:], 0.0).then_inc(ident_made, 1)
            pool.memset(neg_sel[:], 0.0).then_inc(ident_made, 1)
            pool.memset(minus_half[:], -0.5).then_inc(ident_made, 1)
            pool.wait_ge(ident_made, 3)
            pool.affine_select(out=ident[:], in_=ident[:], compare_op=ALU.not_equal, fill=1.0, base=0,
                               pattern=[[-1, P]], channel_multiplier=1).then_inc(ident_made, 1)
            pool.affine_select(out=neg_sel[:], in_=neg_sel[:], compare_op=ALU.not_equal, fill=-1.0, base=0,
                               pattern=[[1, NH], [0, P]], channel_multiplier=-1).then_inc(ident_made, 1)
            pool.memset(ones_row[:], 1.0)
            pool.memset(pool_spare[:], 1.0)
            pool.memset(dve_spare[:], 1.0)
            pool.memset(vx[:, :, :, DH:DH + 1], 1.0)
            pool.memset(g_rows[:], 0.0).then_inc(zeros_made, 1)
            me = Engine(pool, "gpsimd")

            def rsqrt(dst, var, eps, n):
                me.link(pool.tensor_scalar(dst, var, 1.0, eps, ALU.mult, ALU.add))
                return pool.tensor_tensor(dst, dst, minus_half[:, 0:n], ALU.pow)

            def xs(p, b):
                g = slice(b * T, (b + 1) * T)
                pool.wait_ge(x_var, 2 * p + b + 1)
                carry(pool)
                rsqrt(rstd[:, g], mv[:, g, 1], EPS_X, T).then_inc(x_rstd, 1)

            def marg(p, b, half):
                for h in (2 * half, 2 * half + 1):
                    pool.wait_ge(dec_made, 8 * p + 4 * b + h + 1)
                    carry(pool)
                    pool.affine_select(out=dec[:, h, 0:2], in_=dec[:, h, 0:2], compare_op=ALU.is_ge, fill=0.0,
                                       base=0, pattern=[[0, 2], [1, P]], channel_multiplier=-1).then_inc(dec_ready, 1)

            def tail_a(p, b):
                pool.wait_ge(u_var, 2 * p + b + 1)
                carry(pool)
                pool.tensor_tensor(urstd[:, b], uvar[:, b], minus_half[:], ALU.pow).then_inc(u_rstd, 1)

            def tail_b(p, b):
                g = slice(b * T, (b + 1) * T)
                pool.wait_ge(x1_ready, 2 * p + b + 1)
                carry(pool)
                me.link(rsqrt(r1[:, g], mv1[:, g, 1], EPS_X, T))
                me.link(pool.tensor_tensor(rtmp[:, g], r1[:, g], r1[:, g], ALU.mult))
                me.link(pool.tensor_tensor(rtmp[:, g], rtmp[:, g], mv1[:, g, 1], ALU.mult), alone=True)
                me.link(rsqrt(r2[:, g], rtmp[:, g], EPS_FFN, T))
                me.link(pool.tensor_tensor(r2[:, g], r2[:, g], r1[:, g], ALU.mult), alone=True)
                pool.tensor_scalar(rp1[:, g], r1[:, g], 1.0, 1.0, ALU.mult, ALU.add)
                me.link(pool.tensor_scalar(rtmp[:, g], mv1[:, g, 0], -1.0, 0.0, ALU.mult, ALU.add))
                pool.tensor_tensor(rtmp[:, g], rtmp[:, g], r1[:, g], ALU.mult).then_inc(x1_rstd, 1)

            def x12_step(p, b):
                wait(pool, stored[b], 16 * p)
                carry(pool)
                pool.wait_ge(x1_rstd, 2 * p + b + 1)
                carry(pool)
                for t in range(T):
                    g = b * T + t
                    ins = pool.tensor_scalar(x12[:, g], x1[:, g], rp1[:, g:g + 1], rtmp[:, g:g + 1], ALU.mult, ALU.add)
                me.link(ins)
                g = slice(b * T, (b + 1) * T)
                pool.wait_ge(consts_in, N_CONST)
                pool.tensor_tensor(x12[:, g], x12[:, g], o_bias[:], ALU.add).then_inc(x12_ready, 1)

            def pn(p, b, s):
                pool.wait_ge(inv_ready, 8 * p + 4 * b + s + 1)
                carry(pool)
                for u in range(2):
                    ins = pool.tensor_scalar(prob[:, b, s, u], prob[:, b, s, u], p_inv[:, b, s, u:u + 1], 1.0, ALU.mult, ALU.mult)
                ins.then_inc(prob_ready, 1)

            me.walk(dict(xs=xs, marg=marg, tail_a=tail_a, tail_b=tail_b, x12=x12_step, pn=pn))

        @block.vector
        def _(dve):
            me = Engine(dve, "vector")
            dve.wait_ge(zeros_made, 2)
            for tile in (n0[TE:P, :, 3 * TE:S], a0[TE:P, :, 3 * TE:S], q0[:], q1[:], q23[:], gate_w[:]):
                last = dve.memset(tile, 0.0)
            last.then_inc(consts_ready, 1)
            dve.wait_ge(consts_in, N_CONST)
            dve.wait_ge(consts_ready, 1)
            for k, col in ((0, 0), (1, F_ROW)):
                dve.tensor_copy(gate_w[:, 0:C, col:col + NH], gate_raw[:, k, 0:C])
                dve.tensor_tensor(gate_w[:, C:2 * C, col:col + NH], gate_raw[:, k, C:2 * C], gate_raw[:, k, 2 * C:3 * C], ALU.add)
            dve.tensor_scalar(qb_s[:], qb[:], ATT_SCALE, None, ALU.mult).then_inc(consts_ready, 1)

            def xs(p, b):
                dve.wait_ge(x_loaded, 16 * p + 16)
                for g in (b * T, b * T + 1):
                    ins = dve.bn_stats(stat[:, g], x_in[:, g])
                me.link(ins, alone=True)
                for g in (b * T, b * T + 1):
                    ins = dve.bn_aggr(mv[:, g], stat[:, g])
                ins.then_inc(x_var, 1)

            def xq_step(p, b):
                dve.wait_ge(x_rstd, 2 * p + b + 1)
                wait(dve, n_ready, 2 * p)
                for g in (b * T, b * T + 1):
                    ins = dve.tensor_scalar(xq[:, g], x_in[:, g], mv[:, g, 0:1], rstd[:, g:g + 1], ALU.subtract, ALU.mult)
                ins.then_inc(xq_ready, 1)

            def gate(p):
                me.bank_filled()
                dve.tensor_scalar(ig[:], me.bank[0:NH], gate_b[0:NH], None, ALU.add)
                dve.tensor_scalar(fg[:], me.bank[F_ROW:F_ROW + NH], gate_b[F_ROW:F_ROW + NH], None, ALU.add).then_inc(fg_ready, 1)

            def scan(p):
                dve.wait_ge(ln_ready, p + 1)
                me.link(dve.scalar_tensor_tensor(out=fg[:], in0=fg[:], scalar=0.0, in1=ltmp[:], op0=ALU.min, op1=ALU.subtract))
                for b in range(PB):
                    w = slice(b * S, (b + 1) * S)
                    ins = dve.tensor_tensor_scan(cs[:, w], ones_row[:], fg[:, w], 0.0, ALU.mult, ALU.add)
                me.link(ins)
                wait(dve, dec_made, 8 * p)
                me.link(dve.tensor_tensor(g_rows[0:NH], ig[:], cs[:], ALU.subtract))
                for b in range(PB):
                    w = slice(b * S, (b + 1) * S)
                    ins = dve.tensor_tensor_scan(g_max[:, w], g_rows[0:NH, w], g_rows[0:NH, w], -3.0e38, ALU.max, ALU.max)
                me.link(ins)
                dve.tensor_tensor(g_rows[F_ROW:F_ROW + NH], cs[:], g_max[:], ALU.add).then_inc(rows_ready, 1)

            def marg(p, b, half):
                me.bank_filled()
                dve.wait_ge(cols_ready, p + 1)
                for k in range(2):
                    h = 2 * half + k
                    dve.tensor_scalar(dec[:, h, 0:3:2], me.bank[:, k * S:(k + 1) * S].rearrange("p (t q) -> p t q", t=T),
                                      g_col[:, b * T, h:h + 1], 0.0, ALU.add, ALU.min)
                    dve.tensor_scalar(dec[:, h, 1], me.bank[:, k * S + P:(k + 1) * S],
                                      g_col[:, b * T + 1, h:h + 1], 0.0, ALU.add, ALU.min).then_inc(arg_made, 1)

            def sx(p, b, h):
                me.bank_filled()
                dve.wait_ge(dec_ready, 8 * p + 4 * b + h + 1)
                wait(dve, u_ready, 8 * p + 4 * b + h - 3)
                dve.scalar_tensor_tensor(out=cmat[:, h].rearrange("p a b -> p (a b)"), in0=me.bank[:, 0:3 * P], scalar=QK_SCALE,
                                         in1=dec[:, h].rearrange("p a b -> p (a b)"), op0=ALU.mult, op1=ALU.mult).then_inc(c_ready, 1)

            def tail_a(p, b):
                dve.wait_ge(u_ready, 8 * p + 4 * b + 4)
                n = T * NH
                for t in range(T):
                    for h in range(NH):
                        ins = dve.bn_stats(ustat[:, b * n + t * NH + h], um[:, b * T + t, h, 0:DH])
                s = um[:, b * T:(b + 1) * T, :, DH:DH + 1].rearrange("p t h o -> p (t h o)")
                un, ut = unorm[:, b], utmp[:, b]
                me.link(dve.tensor_copy(ut, s))
                me.link(dve.scalar_tensor_tensor(out=un, in0=ut, scalar=-1.0, in1=ut, op0=ALU.mult, op1=ALU.max))
                dve.wait_ge(cols_ready, p + 1)
                me.link(dve.tensor_tensor(un, un, e_col[:, b * T:(b + 1) * T].rearrange("p t h -> p (t h)"), ALU.max))
                me.link(dve.tensor_scalar(un, un, EPS_GATE, None, ALU.add))
                me.link(dve.scalar_tensor_tensor(out=ut, in0=un, scalar=EPS_HEAD, in1=un, op0=ALU.mult, op1=ALU.mult), alone=True)
                for k in range(n):
                    ins = dve.bn_aggr(umv[:, b * n + k], ustat[:, b * n + k])
                me.link(ins)
                dve.tensor_tensor(uvar[:, b], ut, umv[:, b * n:(b + 1) * n, 1], ALU.add).then_inc(u_var, 1)

            def tail_b(p, b):
                n = T * NH
                dve.wait_ge(u_rstd, 2 * p + b + 1)
                wait(dve, x12_ready, 2 * p - 1 + b)
                for t in range(T):
                    for h in range(NH):
                        k = t * NH + h
                        ins = dve.tensor_scalar(x1[:, b * T + t, h * DH:(h + 1) * DH], um[:, b * T + t, h, 0:DH],
                                                umv[:, b * n + k, 0:1], urstd[:, b, k:k + 1], ALU.subtract, ALU.mult)
                me.link(ins)
                for g in (b * T, b * T + 1):
                    ins = dve.tensor_tensor(x1[:, g], x1[:, g], on_row[:], ALU.mult)
                me.link(ins)
                dve.wait_ge(xres_loaded, 16 * p + 16)
                g = slice(b * T, (b + 1) * T)
                me.link(dve.tensor_tensor(x1[:, g], x1[:, g], x_res[:, g], ALU.add))
                for g in (b * T, b * T + 1):
                    ins = dve.bn_stats(stat1[:, g], x1[:, g])
                me.link(ins, alone=True)
                for g in (b * T, b * T + 1):
                    ins = dve.bn_aggr(mv1[:, g], stat1[:, g])
                ins.then_inc(x1_ready, 1)

            def tail_c(p, b):
                dve.wait_ge(x1_rstd, 2 * p + b + 1)
                dve.wait_ge(xqt_ready, 4 * p + 4)
                for g in (b * T, b * T + 1):
                    ins = dve.tensor_scalar(xn[:, g], x1[:, g], mv1[:, g, 0:1], r2[:, g:g + 1], ALU.subtract, ALU.mult)
                ins.then_inc(xn_ready, 1)

            def s_step(p, b, s):
                me.bank_filled()
                dve.tensor_reduce(neg_max[:, b, s], me.bank[:].rearrange("p (u k) -> p u k", u=2), AX.X, ALU.max,
                                  negate=True).then_inc(max_ready, 1)

            def pn(p, b, s):
                dve.wait_ge(exp_done, 8 * p + 4 * b + s + 1)
                dve.reciprocal(p_inv[:, b, s], p_sum[:, b, s]).then_inc(inv_ready, 1)

            def pv0(p, b):
                me.bank_filled()
                v = me.bank[:].rearrange("p (s u q) -> p s u q", s=2, u=2)
                dve.tensor_scalar(a0[0:FH, b].rearrange("p (s q) -> p s q", s=2), v[0:FH, :, 0], vb[0:FH, 0:1], None, ALU.add)
                dve.tensor_scalar(a0[FH:P, b, 0:P], v[FH:P, 0, 1], vb[FH:P, 0:1], None, ALU.add)
                dve.tensor_scalar(a0[FH:P, b, P:P + TE], v[FH:P, 1, 1, 0:TE], vb[FH:P, 0:1], None, ALU.add).then_inc(a_ready, 1)

            def pv1(p, b):
                me.bank_filled()
                v = me.bank[:, 0:S].rearrange("p (u q) -> p u q", u=2)
                w = me.bank[:, S:2 * S].rearrange("p (c u q) -> p c u q", c=2, u=2)
                for u in range(2):
                    rows = slice(u * FH, (u + 1) * FH)
                    dve.tensor_scalar(a1[rows, b], v[rows, u], vb[rows, 1:2], None, ALU.add)
                    for c in range(2):
                        ins = dve.tensor_scalar(a23[rows, b, c], w[rows, c, u], vb[rows, 2 + c:3 + c], None, ALU.add)
                ins.then_inc(a_ready, 1)

            def o(p, b, t):
                me.bank_filled()
                dve.wait_ge(x12_ready, 2 * p + b + 1)
                for k in range(2):
                    e = 2 * t + k
                    rows = slice(k * TE, (k + 1) * TE)
                    ins = dve.tensor_tensor(x12[rows, b * T + t, 0:D >> e], x12[rows, b * T + t, 0:D >> e], me.bank[rows, 0:D >> e], ALU.add)
                ins.then_inc(o_added, 1)

            me.walk(dict(xs=xs, xq=xq_step, gate=gate, scan=scan, marg=marg, sx=sx, tail_a=tail_a, tail_b=tail_b, tail_c=tail_c,
                         s=s_step, pn=pn, pv0=pv0, pv1=pv1, o=o))

        @block.scalar
        def _(act):
            me = Engine(act, "scalar")

            def copy(dst, src):
                return act.activation(dst, src, ACT.Copy)

            def add(dst, src, bias, scale=1.0):
                return act.activation(dst, src, ACT.Identity, bias=bias, scale=scale)

            def xt(p, b, cc):
                me.bank_filled()
                wait(act, c_ready, 8 * p)
                copy(xq_t[:, 2 * cc:2 * cc + 2, b], me.bank[:].rearrange("p (c i) -> p c i", c=2)).then_inc(xqt_ready, 1)

            def lsg(p):
                act.wait_ge(fg_ready, p + 1)
                me.link(act.activation(ltmp[:], fg[:], ACT.Abs))
                me.link(act.activation(ltmp[:], ltmp[:], ACT.Exp, scale=-1.0))
                act.activation(ltmp[:], ltmp[:], ACT.Ln, bias=1.0).then_inc(ln_ready, 1)

            def cols(p):
                me.bank_filled()
                wait(act, x1_ready, 2 * p)
                v = me.bank[:].rearrange("p (g r) -> p g r", g=PB * T)
                copy(g_col[:], v[:, :, 0:NH])
                act.activation(e_col[:], v[:, :, F_ROW:F_ROW + NH], ACT.Exp, scale=-1.0).then_inc(cols_ready, 1)
                act.wait_ge(cols_ready, p + 1)

            def marg(p, b, half):
                for h in (2 * half, 2 * half + 1):
                    act.wait_ge(arg_made, 8 * p + 4 * b + h + 1)
                    act.activation(dec[:, h], dec[:, h], ACT.Exp).then_inc(dec_made, 1)

            def u(p, b, h):
                me.bank_filled()
                if h == 0:
                    wait(act, x1_ready, 2 * p - 1 + b)
                v = me.bank[:].rearrange("p (t n) -> p t n", t=T)[:, :, 0:DH + 1]
                copy(um[:, b * T:(b + 1) * T, h], v).then_inc(u_ready, 1)

            def nt(p, k):
                me.bank_filled()
                wait(act, v_ready, 4 * p)
                if k == 0:
                    v = me.bank[:].rearrange("p (b i) -> p b i", b=PB)
                    add(n0[0:TE], v[0:TE], nb[0:TE, 0:1], nw[0:TE, 0:1])
                    add(n0[TE:P, :, 0:3 * TE], v[TE:P, :, 0:3 * TE], nb[TE:P, 0:1], nw[TE:P, 0:1]).then_inc(n_ready, 1)
                else:
                    add(n1[:].rearrange("p b i -> p (b i)"), me.bank[:, 0:S], nb[:, 1:2], nw[:, 1:2])
                    for c in range(2):
                        ins = add(n2[:, c].rearrange("p b i -> p (b i)"), me.bank[:, S + c * P:S + (c + 1) * P], nb[:, 2 + c:3 + c], nw[:, 2 + c:3 + c])
                    ins.then_inc(n_ready, 1)

            def k_step(p, c):
                me.bank_filled()
                add(kt[:, c].rearrange("p b i -> p (b i)"), me.bank[:], kb[:, c:c + 1]).then_inc(k_ready, 1)

            def q0_step(p):
                me.bank_filled()
                for k in range(2):
                    rows = slice(k * FH, (k + 1) * FH)
                    ins = add(q0[rows, k].rearrange("p b i -> p (b i)"), me.bank[rows], qb_s[rows, 0:1], ATT_SCALE)
                ins.then_inc(q_ready, 1)

            def q1_step(p):
                me.bank_filled()
                for k in range(2):
                    rows = slice(k * FH, (k + 1) * FH)
                    add(q1[rows, k].rearrange("p b i -> p (b i)"), me.bank[rows, 0:S], qb_s[rows, 1:2], ATT_SCALE)
                for c in range(2):
                    v = me.bank[:, S + c * P:S + (c + 1) * P].rearrange("p (b i) -> p b i", b=PB)
                    for k in range(2):
                        rows = slice(k * FH, (k + 1) * FH)
                        ins = add(q23[rows, c, :, k], v[rows], qb_s[rows, 2 + c:3 + c], ATT_SCALE)
                ins.then_inc(q_ready, 1)

            def v_step(p, b, t):
                me.bank_filled()
                wait(act, a_ready, 4 * p)
                copy(vf[:, b * T + t], me.bank[:]).then_inc(v_ready, 1)

            def s_step(p, b, s):
                act.wait_ge(max_ready, 8 * p + 4 * b + s + 1)
                for k in range(2):
                    ins = act.activation(prob[:, b, s, k], me.bank[:, k * S:(k + 1) * S], ACT.Exp, bias=neg_max[:, b, s, k:k + 1],
                                         accum_out=p_sum[:, b, s, k:k + 1])
                ins.then_inc(exp_done, 1)

            def pt(p, b, s):
                me.bank_filled()
                wait(act, a_ready, 4 * p)
                copy(prob_t[:, b, :, s].rearrange("p k u q -> p k (u q)"), me.bank[:].rearrange("p (k n) -> p k n", k=T)).then_inc(probt_ready, 1)

            act.wait_ge(consts_in, N_CONST)
            act.wait_ge(consts_ready, 2)
            act.wait_ge(zeros_made, 2)
            me.walk(dict(xt=xt, lsg=lsg, cols=cols, marg=marg, u=u, nt=nt, k=k_step, q0=q0_step, q1=q1_step, v=v_step, s=s_step, pt=pt))

        @block.tensor
        def _(pe):
            me = Engine(pe, "tensor")

            def mm(dst, lhs, rhs, first, last):
                return pe.matmul(dst, lhs, rhs, start=first, stop=last)

            def xt(p, b, cc):
                me.bank_free()
                pe.wait_ge(xq_ready, 2 * p + b + 1)
                for c in range(2):
                    for t in range(T):
                        n = (c * T + t) * P
                        f = (2 * cc + c) * P
                        ins = pe.transpose(me.bank[:, n:n + P], xq[:, b * T + t, f:f + P], ident[:])
                ins.then_inc(me.ring.filled, 1)

            def gate(p):
                me.bank_free()
                pe.wait_ge(xqt_ready, 4 * p + 4)
                pe.wait_ge(kx_loaded, 16 * p + 16)
                for c in range(C):
                    mm(me.bank[0:F_ROW + NH], gate_w[:, c], xq_t[:, c].rearrange("p b i -> p (b i)"), c == 0, False)
                for c in range(C):
                    ins = mm(me.bank[0:F_ROW + NH].rearrange("p (b i) -> p b i", b=PB), gate_w[:, C + c], kx_t[:, c:PB * C:C], False, c == C - 1)
                ins.then_inc(me.ring.filled, 1)

            def cols(p):
                me.bank_free()
                pe.wait_ge(rows_ready, p + 1)
                for g in range(PB * T):
                    w = slice(g * P, (g + 1) * P)
                    ins = pe.transpose(me.bank[:, w], g_rows[:, w], ident[:])
                ins.then_inc(me.ring.filled, 1)

            def marg(p, b, half):
                me.bank_free()
                pe.wait_ge(rows_ready, p + 1)
                for k in range(2):
                    ins = mm(me.bank[:, k * S:(k + 1) * S], neg_sel[:, 2 * half + k], g_max[:, b * S:(b + 1) * S], True, True)
                ins.then_inc(me.ring.filled, 1)

            def sx(p, b, h):
                me.bank_free()
                k = kx_t[:, b * C + h]
                mm(me.bank[:, 0:4 * P].rearrange("p (n i) -> p n i", n=2)[:, :, 0:P], k[:, 0:P], xq_t[:, h, b].rearrange("p (t i) -> p t i", t=T), True, True)
                mm(me.bank[:, P:2 * P], k[:, P:S], xq_t[:, h, b, P:S], True, True).then_inc(me.ring.filled, 1)

            def u(p, b, h):
                me.bank_free()
                pe.wait_ge(c_ready, 8 * p + 4 * b + h + 1)
                pe.wait_ge(vx_loaded, 64 * p + 64)
                v0, v1 = vx[:, b * T, h], vx[:, b * T + 1, h]
                mm(me.bank[:, 0:DH + 1], cmat[:, h, 0], v0, True, True)
                mm(me.bank[:, S:S + DH + 1], cmat[:, h, 2], v0, True, False)
                mm(me.bank[:, S:S + DH + 1], cmat[:, h, 1], v1, False, True).then_inc(me.ring.filled, 1)

            def nt(p, k):
                me.bank_free()
                pe.wait_ge(xn_ready, 2 * p + 2)
                for b in range(PB):
                    if k == 0:
                        for t in range(T):
                            n = (b * T + t) * P
                            ins = pe.transpose(me.bank[:, n:n + P], xn[:, b * T + t, 0:P], ident[:])
                    else:
                        ins = pe.transpose(me.bank[:, b * P:(b + 1) * P], xn[:, b * T, P:2 * P], ident[:])
                        for c in range(2):
                            n = S + c * P + b * TE
                            ins = pe.transpose(me.bank[:, n:n + TE], xn[0:TE, b * T, (2 + c) * P:(3 + c) * P], ident[0:TE, 0:TE])
                ins.then_inc(me.ring.filled, 1)

            def project(dst, w, c, tokens):
                cols = slice(c * P, (c + 1) * P)
                inputs = [n0, n1, n2[:, 0], n2[:, 1]]
                for k in reversed(range(C)):
                    seen = min(tokens, (S, 2 * TE, TE, TE)[k])
                    src = inputs[k][:, :, 0:seen]
                    ins = pe.matmul(dst[:, :, 0:seen], w[:, k, cols], src, start=k == C - 1, stop=k == 0, skip_group_check=True)
                return ins

            def k_step(p, c):
                me.bank_free()
                pe.wait_ge(n_ready, 2 * p + 2)
                if c == 0:
                    pe.wait_ge(weights_in, 64)
                project(me.bank[:].rearrange("p (b i) -> p b i", b=PB), wk, c, S).then_inc(me.ring.filled, 1)

            def q0_step(p):
                me.bank_free()
                project(me.bank[:].rearrange("p (b i) -> p b i", b=PB), wq, 0, S).then_inc(me.ring.filled, 1)

            def q1_step(p):
                me.bank_free()
                project(me.bank[:, 0:S].rearrange("p (b i) -> p b i", b=PB), wq, 1, 2 * TE)
                for c in range(2):
                    ins = project(me.bank[:, S + c * P:S + (c + 1) * P].rearrange("p (b i) -> p b i", b=PB), wq, 2 + c, TE)
                ins.then_inc(me.ring.filled, 1)

            def v_step(p, b, t):
                me.bank_free()
                if t == 1:
                    ins = mm(me.bank[:], n0[:, b, P:S], wv[:, 0], True, True)
                else:
                    mm(me.bank[:], n0[:, b, 0:P], wv[:, 0], True, False)
                    mm(me.bank[0:TE], n2[:, 0, b], wv[:, 2], False, False)
                    mm(me.bank[0:TE], n2[:, 1, b], wv[:, 3], False, False)
                    ins = mm(me.bank[:], n1[:, b], wv[:, 1], False, True)
                ins.then_inc(me.ring.filled, 1)

            def s_step(p, b, s):
                me.bank_free()
                pe.wait_ge(q_ready, 2 * p + 2)
                pe.wait_ge(k_ready, 4 * p + 4)
                for u in range(2):
                    dst = me.bank[:, u * S:(u + 1) * S]
                    if s < 2:
                        ins = mm(dst, q0[:, u, b, s * P:(s + 1) * P], kt[:, 0, b], True, True)
                    elif s == 2:
                        ins = mm(dst, q1[:, u, b], kt[:, 1, b], True, True)
                    else:
                        ins = mm(dst, q23[:, u, b].rearrange("p k i -> p (k i)"), kt[:, 2 + u, b], True, True)
                ins.then_inc(me.ring.filled, 1)

            def pt(p, b, s):
                me.bank_free()
                pe.wait_ge(prob_ready, 8 * p + 4 * b + s + 1)
                for k in range(T):
                    for u in range(2):
                        n = (k * 2 + u) * P
                        ins = pe.transpose(me.bank[:, n:n + P], prob[:, b, s, u, k * P:(k + 1) * P], ident[:])
                ins.then_inc(me.ring.filled, 1)

            def pv0(p, b):
                me.bank_free()
                pe.wait_ge(probt_ready, 8 * p + 4 * b + 2)
                pe.wait_ge(v_ready, 4 * p + 4)
                for k in range(T):
                    ins = mm(me.bank[:], vf[:, b * T + k, 0:P], prob_t[:, b, k, 0:2].rearrange("p s u q -> p (s u q)"), k == 0, k == T - 1)
                ins.then_inc(me.ring.filled, 1)

            def pv1(p, b):
                me.bank_free()
                pe.wait_ge(probt_ready, 8 * p + 4 * b + 4)
                for k in range(T):
                    mm(me.bank[:, 0:S], vf[:, b * T + k, P:2 * P], prob_t[:, b, k, 2].rearrange("p u q -> p (u q)"), k == 0, k == T - 1)
                for c in range(2):
                    for k in range(T):
                        ins = mm(me.bank[:, S + c * P:S + (c + 1) * P], vf[:, b * T + k, (2 + c) * P:(3 + c) * P], prob_t[:, b, k, 3, c], k == 0, k == T - 1)
                ins.then_inc(me.ring.filled, 1)

            def o(p, b, t):
                me.bank_free()
                pe.wait_ge(a_ready, 4 * p + 2 * b + 2)
                if t == 1:
                    ins = mm(me.bank[:, 0:P], a0[:, b, P:S], wo[:, 0, 0:P], True, True)
                else:
                    mm(me.bank[:], a0[:, b, 0:P], wo[:, 0], True, False)
                    mm(me.bank[0:TE], a23[:, b, 0], wo[:, 2], False, False)
                    mm(me.bank[0:TE], a23[:, b, 1], wo[:, 3], False, False)
                    ins = mm(me.bank[:], a1[:, b], wo[:, 1], False, True)
                ins.then_inc(me.ring.filled, 1)

            pe.wait_ge(ident_made, 5)
            pe.wait_ge(zeros_made, 2)
            pe.wait_ge(consts_ready, 2)
            me.walk(dict(xt=xt, gate=gate, cols=cols, marg=marg, sx=sx, u=u, nt=nt, k=k_step, q0=q0_step, q1=q1_step, v=v_step,
                         s=s_step, pt=pt, pv0=pv0, pv1=pv1, o=o))


_OUT = ((B, S, D), "float32")


def kernel(**inputs):
    import numpy as np
    import concourse.bacc as bacc
    from concourse.bass_utils import run_bass_kernel_spmd as run

    def get(name):
        return np.asarray(inputs[name])

    def column(name):
        return get(name).reshape(C, P).T

    laid = {
        "x": get("x"), "ctx": get("ctx_1024"), "ctx_t": get("ctx_1024").transpose(0, 2, 1),
        "ig_w": get("L0_xattn_igate_kernel"), "ig_b": get("L0_xattn_igate_bias").reshape(NH, 1),
        "fg_w": get("L0_xattn_fgate_kernel"), "fg_b": get("L0_xattn_fgate_bias").reshape(NH, 1),
        "on_scale": get("L0_xattn_outnorm_scale").reshape(1, D),
        "n_w": column("L0_ffn_norm_w"), "n_b": column("L0_ffn_norm_b"),
        "wq_t": get("L0_ffn_q_w").T, "q_b": column("L0_ffn_q_b"), "wk_t": get("L0_ffn_k_w").T, "k_b": column("L0_ffn_k_b"),
        "wv_t": get("L0_ffn_v_w").T, "v_b": column("L0_ffn_v_b"), "wo_t": get("L0_ffn_o_w").T,
        "o_b": get("L0_ffn_o_b").reshape(1, D),
    }
    nc = bacc.Bacc("TRN2", target_bir_lowering=False, num_devices=1)
    arrays, args = {}, []
    for name, a in laid.items():
        arrays[f"in_{name}"] = np.ascontiguousarray(a)
        args.append(nc.dram_tensor(f"in_{name}", a.shape, mybir.dt.from_np(a.dtype), kind="ExternalInput").ap())
    args.append(nc.dram_tensor("out_0", _OUT[0], F32, kind="ExternalOutput").ap())
    xattn_ffn(nc, *args)
    r = run(nc, [arrays], core_ids=[0])
    return r.results[0]["out_0"]
```

```python
from contextlib import ExitStack

import concourse.bass as bass
from concourse import mybir

F32 = mybir.dt.float32
F32R = mybir.dt.float32r
ALU = mybir.AluOpType
ACT = mybir.ActivationFunctionType
AX = mybir.AxisListType

B, S, D = 16, 256, 512
P = 128
PB = 2
PAIRS = B // PB
T = S // P
C = D // P
NH, DH = 4, 128
E = 4
TE = S // E
FH = D // 8
EPS_X, EPS_GATE, EPS_HEAD, EPS_FFN = 1e-5, 1e-6, 1e-6, 1e-5
QK_SCALE = DH ** -0.5
ATT_SCALE = D ** -0.5
SPARE = 16
MASKED = -2.0 ** 100
GT = 32
F_ROW = 32

BODY = [
    ("G", "xs", 0), ("F", "nt", 0), ("F", "nt", 1), ("F", "k", 0), ("F", "q0"), ("F", "k", 1), ("F", "k", 2),
    ("X", "cols", 0), ("F", "x12", 0), ("F", "k", 3), ("F", "q1"), ("X", "cols", 1), ("X", "marg", 0, 0),
    ("F", "v", 0), ("X", "marg", 0, 1), ("F", "s", 0, 0), ("X", "marg", 0, 2), ("F", "x12", 1), ("F", "v", 1),
    ("F", "s", 0, 1), ("X", "sx", 0, 0), ("F", "v", 2), ("X", "sx", 0, 1), ("X", "marg", 0, 3), ("F", "s", 0, 2),
    ("F", "pn", 0, 0), ("X", "u", 0, 0), ("X", "marg", 1, 0), ("F", "v", 3), ("F", "s", 0, 3), ("F", "pn", 0, 1),
    ("X", "sx", 0, 2), ("F", "pn", 0, 2), ("X", "u", 0, 1), ("F", "s", 1, 0), ("F", "pn", 0, 3), ("X", "sx", 0, 3),
    ("F", "pt", 0, 0), ("X", "sx", 1, 0), ("X", "u", 0, 2), ("X", "marg", 1, 1), ("F", "s", 1, 1), ("X", "u", 0, 3),
    ("F", "pn", 1, 0), ("F", "s", 1, 2), ("F", "pt", 0, 1), ("X", "sx", 1, 1), ("F", "pn", 1, 1), ("X", "marg", 1, 2),
    ("X", "u", 1, 0), ("X", "u", 1, 1), ("X", "marg", 1, 3), ("X", "tail_a", 0), ("F", "pt", 0, 2), ("F", "s", 1, 3),
    ("X", "sx", 1, 2), ("X", "sx", 1, 3), ("G", "xs", 1), ("X", "u", 1, 2), ("G", "xq", 0), ("X", "u", 1, 3),
    ("G", "xt", 0, 0), ("F", "pn", 1, 2), ("G", "xt", 0, 1), ("F", "pn", 1, 3), ("F", "pt", 0, 3), ("G", "xq", 1),
    ("F", "pv0", 0), ("X", "tail_a", 1), ("F", "pt", 1, 0), ("X", "tail_b", 0), ("F", "pt", 1, 1), ("F", "pv1", 0),
    ("F", "pt", 1, 2), ("F", "pt", 1, 3), ("X", "tail_b", 1), ("F", "pv0", 1), ("X", "tail_c", 0), ("F", "pv1", 1),
    ("G", "xt", 1, 0), ("G", "xt", 1, 1), ("G", "gate"), ("X", "tail_c", 1), ("G", "gsum"), ("F", "o", 0),
    ("F", "o", 1), ("G", "scan"), ("G", "lsg"),
]
LAG = {"F": 0, "X": 1, "G": 2}
ORDER = {
    "fill2": [s for s in BODY if s[0] == "G"],
    "fill1": [s for s in BODY if s[0] != "F"],
    "body": BODY,
    "drain1": [s for s in BODY if s[0] != "G"],
    "drain2": [s for s in BODY if s[0] == "F"],
}
ROUND = {"fill2": -2, "fill1": -1, "drain1": PAIRS - 2, "drain2": PAIRS - 1}

RING_OF = {
    "nt": "turn", "xt": "turn", "pt": "turn",
    "k": "prod", "q0": "prod", "q1": "prod", "v": "prod", "pv0": "prod", "pv1": "prod", "o": "prod", "u": "prod",
    "s": "attn",
    "gate": "xatt", "gsum": "xatt", "cols": "xatt", "marg": "xatt", "sx": "xatt",
}
OWN = {"vector": {"G": 8, "X": 20, "F": 0}, "scalar": {"G": 2, "X": 0, "F": 0}, "gpsimd": {"G": 4, "X": 16, "F": 2}}


class Ring:

    def __init__(self, name, ctx, nc):
        self.banks = [ctx.enter_context(nc.psum_tensor(f"{name}{k}", [P, 512], F32)) for k in range(2)]
        self.filled = ctx.enter_context(nc.semaphore(f"{name}_filled"))
        self.jobs = {ph: [s for s in ORDER[ph] if RING_OF.get(s[1]) == name] for ph in ORDER}
        assert len(self.jobs["body"]) % 2 == 0

    def place(self, phase, i, step):
        count = {ph: len(self.jobs[ph]) for ph in ORDER}
        n = self.jobs[phase].index(step) + 1
        if phase != "fill2":
            n += count["fill2"]
        if phase not in ("fill2", "fill1"):
            n += count["fill1"]
        if phase == "drain2":
            n += count["drain1"]
        rounds = {"body": i, "drain1": PAIRS - 2, "drain2": PAIRS - 2}.get(phase, 0)
        return self.banks[(n - 1) % 2], rounds * count["body"] + n

    def before(self, phase, i, step):
        ago = 2
        n = self.jobs[phase].index(step)
        while n < ago:
            ago -= n
            if phase == "fill2":
                return None
            if phase == "body" and isinstance(i, int) and i == 0:
                phase, i = "fill1", -1
            elif phase == "body":
                i = i - 1
            else:
                phase = {"fill1": "fill2", "drain1": "body", "drain2": "drain1"}[phase]
                i = {"fill2": -2, "body": PAIRS - 3, "drain1": PAIRS - 2}[phase]
            n = len(self.jobs[phase])
        before = self.jobs[phase][n - ago]
        return before, i + LAG[before[0]]


def xattn_ffn(nc, x, ctx_in, ctx_t, ig_w, ig_b, fg_w, fg_b, on_scale, n_w, n_b,
              wq_t, q_b, wk_t, k_b, wv_t, v_b, wo_t, o_b, out):
    ctx = ExitStack()
    with ctx:
        def sb(name, shape, dtype=F32):
            return ctx.enter_context(nc.sbuf_tensor(name, shape, dtype))

        def sem(name):
            return ctx.enter_context(nc.semaphore(name))

        rings = {n: Ring(n, ctx, nc) for n in ("turn", "prod", "attn", "xatt")}

        ident = sb("ident", [P, P])
        neg_sel = sb("neg_sel", [F_ROW + NH, NH, P], F32R)
        ident_r = sb("ident_r", [P, P], F32R)
        mask = sb("mask", [P, 2, P], F32R)
        wq, wk, wv, wo = (sb(n, [P, C, D]) for n in ("wq", "wk", "wv", "wo"))
        gate_raw = sb("gate_raw", [P, 2, 3 * C, NH])
        gate_w = sb("gate_w", [P, 2 * C, GT])
        gate_sel = sb("gate_sel", [P, F_ROW + NH])
        gate_part = sb("gate_part", [P, PB * S])
        gate_b = sb("gate_b", [F_ROW + NH, 1])
        on_row = sb("on_row", [P, D])
        o_bias = sb("o_bias", [P, T, D])
        qb, kb, vb, nw, nb = (sb(n, [P, C]) for n in ("qb", "kb", "vb", "nw", "nb"))
        qb_s = sb("qb_s", [P, C])
        pool_spare, dve_spare = sb("pool_spare", [1, SPARE + 1]), sb("dve_spare", [1, SPARE + 1])
        minus_half = sb("minus_half", [P, 8])
        ones_row = sb("ones_row", [NH, S])
        x_in = sb("x_in", [P, PB * T, D])
        x_res = sb("x_res", [P, PB * T, D])
        xn = sb("xn", [P, PB * T, D])
        xq_t = sb("xq_t", [P, C, PB, S])
        kx_t = sb("kx_t", [P, PB * C, S])
        vx = sb("vx", [P, PB * T, NH, DH + 1])
        stat = sb("stat", [P, PB * T, 6])
        mv = sb("mv", [P, PB * T, 2])
        rstd = sb("rstd", [P, PB * T])
        x_off = sb("x_off", [P, PB * T])
        fg = sb("fg", [NH, PB * S])
        ltmp = gate_part[0:NH]
        cs = sb("cs", [NH, PB * S])
        g_rows = sb("g_rows", [P, PB * S])
        g_max = sb("g_max", [NH, PB * S])
        g_part = sb("g_part", [F_ROW + NH, PB * S], F32R)
        g_col = sb("g_col", [P, PB * T, NH])
        e_col = sb("e_col", [P, PB * T, NH])
        dec = sb("dec", [P, NH, 3, P])
        neg_sel0 = dec[0:F_ROW + NH, :, 0]
        mask0 = dec[:, :, 1][:, 0:2]
        cmat = sb("cmat", [P, NH, 3, P])
        um = sb("um", [P, PB * T, NH, DH + 1])
        ustat = sb("ustat", [P, PB * T * NH, 6])
        umv = sb("umv", [P, PB * T * NH, 2])
        unorm = sb("unorm", [P, PB, T * NH])
        utmp = sb("utmp", [P, PB, T * NH])
        uvar = sb("uvar", [P, PB, T * NH])
        urstd = sb("urstd", [P, PB, T * NH])
        x1 = sb("x1", [P, PB * T, D])
        stat1 = sb("stat1", [P, PB * T, 6])
        mv1 = sb("mv1", [P, PB * T, 2])
        r1 = sb("r1", [P, PB * T])
        rp1 = sb("rp1", [P, PB * T])
        r2 = sb("r2", [P, PB * T])
        rtmp = sb("rtmp", [P, PB * T])
        n0 = sb("n0", [P, PB, S])
        n1 = sb("n1", [P, PB, 2 * TE])
        n2 = sb("n2", [P, 2, PB, TE])
        kt = sb("kt", [P, C, PB, S])
        q0 = sb("q0", [P, 2, PB, S])
        q1 = sb("q1", [P, 2, PB, 2 * TE])
        q23 = sb("q23", [P, 2, PB, 2, TE])
        vf = sb("vf", [P, PB * T, D])
        neg_max = sb("neg_max", [P, PB, 4, 2])
        p_sum = sb("p_sum", [P, PB, 4, 2])
        p_inv = sb("p_inv", [P, PB, 4, 2])
        prob = sb("prob", [P, PB, 4, 2, S])
        prob_t = sb("prob_t", [P, PB, T, 4, 2, P])
        a0 = sb("a0", [P, PB, S])
        a1 = sb("a1", [P, PB, 2 * TE])
        a23 = sb("a23", [P, PB, 2, TE])
        x12 = sb("x12", [P, PB * T, D])

        consts_in, weights_in = sem("consts_in"), sem("weights_in")
        ident_made = sem("ident_made")
        zeros_made = sem("zeros_made")
        consts_ready = sem("consts_ready")
        x_loaded, kx_loaded, vx_loaded, xres_loaded = (sem(n) for n in ("x_loaded", "kx_loaded", "vx_loaded", "xres_loaded"))
        stored = [sem(f"stored{b}") for b in range(PB)]
        x_var = sem("x_var")
        x_off_ready = sem("x_off_ready")
        xq_ready = sem("xq_ready")
        xqt_ready = sem("xqt_ready")
        gpart_ready = sem("gpart_ready")
        ln_ready = sem("ln_ready")
        rows_ready = sem("rows_ready")
        cols_ready = sem("cols_ready")
        dec_ready = sem("dec_ready")
        c_ready = sem("c_ready")
        u_ready = sem("u_ready")
        u_var = sem("u_var")
        u_rstd = sem("u_rstd")
        x1_ready = sem("x1_ready")
        x1_rstd = sem("x1_rstd")
        xn_ready = sem("xn_ready")
        n_ready = sem("n_ready")
        k_ready = sem("k_ready")
        q_ready = sem("q_ready")
        v_ready = sem("v_ready")
        max_ready = sem("max_ready")
        exp_done = sem("exp_done")
        inv_ready = sem("inv_ready")
        prob_ready = sem("prob_ready")
        probt_ready = sem("probt_ready")
        a_ready = sem("a_ready")
        x12_ready = sem("x12_ready")
        o_added = sem("o_added")
        own = {e: {s: sem(f"own_{e}_{s}") for s in LAG} for e in OWN}

        READ = {
            "xt": lambda b, cc: (xqt_ready, 4, 2 * b + cc + 1), "nt": lambda k: (n_ready, 2, k + 1),
            "pt": lambda b, s: (probt_ready, 8, 4 * b + s + 1),
            "k": lambda c: (k_ready, 4, c + 1), "q0": lambda: (q_ready, 2, 1), "q1": lambda: (q_ready, 2, 2),
            "v": lambda k: (v_ready, 4, k + 1), "o": lambda k: (o_added, 2, k + 1),
            "pv0": lambda b: (a_ready, 4, 2 * b + 1), "pv1": lambda b: (a_ready, 4, 2 * b + 2),
            "u": lambda b, h: (u_ready, 8, 4 * b + h + 1), "s": lambda b, s: (exp_done, 8, 4 * b + s + 1),
            "gate": lambda: (gpart_ready, 1, 1), "gsum": lambda: (rows_ready, 1, 1), "cols": lambda b: (cols_ready, 2, b + 1),
            "marg": lambda b, h: (dec_ready, 8, 4 * b + h + 1), "sx": lambda b, h: (c_ready, 8, 4 * b + h + 1),
        }

        def wait(eng, s, n):
            if not isinstance(n, int) or n > 0:
                eng.wait_ge(s, n)

        carried = [0]

        def carry(eng):
            carried[0] = k = carried[0] % SPARE + 1
            if eng.engine == nc.gpsimd.engine:
                eng.tensor_tensor(pool_spare[:, k:k + 1], pool_spare[:, 0:1], pool_spare[:, 0:1], ALU.mult)
            else:
                eng.tensor_copy(dve_spare[:, k:k + 1], dve_spare[:, 0:1])

        class Engine:

            def __init__(self, eng, name):
                self.eng, self.name = eng, name

            def link(self, ins, alone=False):
                s = own[self.name][self.stage]
                self.count[self.stage] += 1
                ins.then_inc(s, 1)
                self.eng.wait_ge(s, self.p * OWN[self.name][self.stage] + self.count[self.stage])
                if alone:
                    carry(self.eng)

            def run(self, steps, phase, i):
                self.count = dict.fromkeys(LAG, 0)
                for step in ORDER[phase]:
                    self.stage, what, *args = step
                    self.p = i + LAG[self.stage]
                    if what in RING_OF:
                        self.ring = rings[RING_OF[what]]
                        self.bank, self.fills = self.ring.place(phase, i, step)
                        self.before = self.ring.before(phase, i, step)
                    if what in steps:
                        steps[what](self.p, *args)
                for s in LAG if self.name in OWN else ():
                    if any(step[0] == s for step in ORDER[phase]):
                        assert self.count[s] == OWN[self.name][s], (self.name, s, self.count[s])

            def walk(self, steps):
                for phase in ("fill2", "fill1"):
                    self.run(steps, phase, ROUND[phase])
                self.run(steps, "body", 0)
                with self.eng.Fori(1, PAIRS - 2) as i:
                    self.run(steps, "body", i)
                for phase in ("drain1", "drain2"):
                    self.run(steps, phase, ROUND[phase])

            def bank_filled(self):
                self.eng.wait_ge(self.ring.filled, self.fills)

            def bank_free(self):
                if self.before is not None:
                    (_, what, *args), pair = self.before
                    s, per_pair, n = READ[what](*args)
                    self.eng.wait_ge(s, pair * per_pair + n)

        x_d = x.rearrange("(p b) (t q) d -> p q (b t) d", b=PB, q=P)
        ctx_d = ctx_in.rearrange("(p b) (t q) d -> p q (b t) d", b=PB, q=P)
        ctxt_d = ctx_t.rearrange("(p b) (c q) i -> p q (b c) i", b=PB, q=P)
        out_d = out.rearrange("p (t q) d -> p q t d", q=P)

        block = ctx.enter_context(nc.Block())

        @block.sync
        def _(sp):
            def load_x(p):
                sp.dma_start(x_in[:], x_d[p]).then_inc(x_loaded, 16)

            def load_kx(p):
                sp.dma_start(kx_t[:], ctxt_d[p]).then_inc(kx_loaded, 16)

            def load_vx(p):
                for g in range(PB * T):
                    sp.dma_start(vx[:, g, :, 0:DH], ctx_d[p, :, g, :].rearrange("q (h d) -> q h d", h=NH)).then_inc(vx_loaded, 16)

            def load_xres(p):
                sp.dma_start(x_res[:], x_d[p]).then_inc(xres_loaded, 16)

            def store(p, b):
                sp.wait_ge(o_added, 2 * p + 2)
                sp.dma_start(out_d[p * PB + b], x12[:, b * T:(b + 1) * T, :]).then_inc(stored[b], 16)

            load_x(0)
            sp.wait_ge(zeros_made, 1)
            for n, (tile, w) in enumerate(((gate_raw[:, 0], ig_w), (gate_raw[:, 1], fg_w))):
                sp.dma_start(tile, w.rearrange("(c p) h -> p c h", p=P)).then_inc(consts_in, 16)
            sp.dma_start(gate_b[0:NH], ig_b).then_inc(consts_in, 16)
            sp.dma_start(gate_b[F_ROW:F_ROW + NH], fg_b).then_inc(consts_in, 16)
            for tile, v in ((qb, q_b), (kb, k_b), (vb, v_b), (nw, n_w), (nb, n_b)):
                sp.dma_start(tile[:], v).then_inc(consts_in, 16)
            sp.dma_start(on_row[:], on_scale.partition_broadcast(P)).then_inc(consts_in, 16)
            for e in range(E):
                rows = slice(TE * (e % 2), TE * (e % 2 + 1))
                sp.dma_start(o_bias[rows, e // 2, 0:D >> e], o_b[:, 0:D >> e].partition_broadcast(TE)).then_inc(consts_in, 16)
            load_kx(0)
            load_vx(0)
            load_xres(0)
            for tile, w in ((wk, wk_t), (wq, wq_t), (wv, wv_t), (wo, wo_t)):
                sp.dma_start(tile[:], w.rearrange("(c p) n -> p c n", p=P)).then_inc(weights_in, 16)

            def reload(p):
                sp.wait_ge(c_ready, 8 * p)
                load_kx(p)
                sp.wait_ge(u_ready, 8 * p)
                load_vx(p)

            def reload_x(p):
                sp.wait_ge(xqt_ready, 4 * p)
                load_x(p)

            def reload_xres(p):
                sp.wait_ge(x1_ready, 2 * p)
                load_xres(p)

            reload_x(1)
            reload(1)
            reload_x(2)
            reload_xres(1)
            with sp.Fori(0, PAIRS - 3) as i:
                reload(i + 2)
                reload_x(i + 3)
                reload_xres(i + 2)
                store(i, 0)
                store(i, 1)
            reload(PAIRS - 1)
            reload_xres(PAIRS - 1)
            for p in (PAIRS - 3, PAIRS - 2, PAIRS - 1):
                store(p, 0)
                store(p, 1)
            for b in range(PB):
                sp.wait_ge(stored[b], 16 * PAIRS)

        N_CONST = 16 * 14

        @block.gpsimd
        def _(pool):
            pool.memset(gate_b[:], 0.0)
            pool.memset(o_bias[:], 0.0).then_inc(zeros_made, 1)
            pool.memset(ident[:], 0.0).then_inc(ident_made, 1)
            pool.memset(neg_sel0, 0.0).then_inc(ident_made, 1)
            pool.memset(gate_sel[:], 0.0).then_inc(ident_made, 1)
            pool.memset(minus_half[:], -0.5).then_inc(ident_made, 1)
            pool.wait_ge(ident_made, 4)
            pool.affine_select(out=ident[:], in_=ident[:], compare_op=ALU.not_equal, fill=1.0, base=0,
                               pattern=[[-1, P]], channel_multiplier=1).then_inc(ident_made, 1)
            for k in range(2):
                pool.affine_select(out=neg_sel0, in_=neg_sel0, compare_op=ALU.not_equal, fill=-1.0, base=F_ROW * k,
                                   pattern=[[1, NH], [0, P]], channel_multiplier=-1).then_inc(ident_made, 1)
                pool.wait_ge(ident_made, 6 + k)
            n = 7
            for c in range(C):
                for k in range(2):
                    pool.affine_select(out=gate_sel[:, F_ROW * k:F_ROW * k + NH], in_=gate_sel[:, F_ROW * k:F_ROW * k + NH],
                                       compare_op=ALU.not_equal, fill=1.0, base=GT * c + NH * k,
                                       pattern=[[1, NH]], channel_multiplier=-1).then_inc(ident_made, 1)
                n += 2
                pool.wait_ge(ident_made, n)
            pool.memset(mask0, 0.0).then_inc(ident_made, 1)
            pool.wait_ge(ident_made, n + 1)
            pool.affine_select(out=mask0, in_=mask0, compare_op=ALU.is_ge, fill=MASKED, base=0,
                               pattern=[[0, 2], [1, P]], channel_multiplier=-1).then_inc(ident_made, 1)
            pool.memset(ones_row[:], 1.0)
            pool.memset(pool_spare[:], 1.0)
            pool.memset(dve_spare[:], 1.0)
            pool.memset(vx[:, :, :, DH:DH + 1], 1.0)
            pool.memset(g_rows[:], 0.0).then_inc(zeros_made, 1)
            me = Engine(pool, "gpsimd")

            def rsqrt(dst, var, eps, n):
                me.link(pool.tensor_scalar(dst, var, 1.0, eps, ALU.mult, ALU.add))
                return pool.tensor_tensor(dst, dst, minus_half[:, 0:n], ALU.pow)

            def xs(p, b):
                g = slice(b * T, (b + 1) * T)
                pool.wait_ge(x_var, 2 * p + b + 1)
                carry(pool)
                pool.tensor_scalar(x_off[:, g], mv[:, g, 0], -1.0, 0.0, ALU.mult, ALU.add)
                me.link(rsqrt(rstd[:, g], mv[:, g, 1], EPS_X, T))
                pool.tensor_tensor(x_off[:, g], x_off[:, g], rstd[:, g], ALU.mult).then_inc(x_off_ready, 1)

            def xq_step(p, b):
                pool.wait_ge(x_off_ready, 2 * p + b + 1)
                carry(pool)
                for g in (b * T, b * T + 1):
                    ins = pool.tensor_scalar(x_in[:, g], x_in[:, g], rstd[:, g:g + 1], x_off[:, g:g + 1], ALU.mult, ALU.add)
                ins.then_inc(xq_ready, 1)

            def tail_a(p, b):
                pool.wait_ge(u_var, 2 * p + b + 1)
                carry(pool)
                pool.tensor_tensor(urstd[:, b], uvar[:, b], minus_half[:], ALU.pow).then_inc(u_rstd, 1)

            def tail_b(p, b):
                g = slice(b * T, (b + 1) * T)
                pool.wait_ge(x1_ready, 2 * p + b + 1)
                carry(pool)
                me.link(rsqrt(r1[:, g], mv1[:, g, 1], EPS_X, T))
                me.link(pool.tensor_tensor(rtmp[:, g], r1[:, g], r1[:, g], ALU.mult))
                me.link(pool.tensor_tensor(rtmp[:, g], rtmp[:, g], mv1[:, g, 1], ALU.mult), alone=True)
                me.link(rsqrt(r2[:, g], rtmp[:, g], EPS_FFN, T))
                me.link(pool.tensor_tensor(r2[:, g], r2[:, g], r1[:, g], ALU.mult), alone=True)
                pool.tensor_scalar(rp1[:, g], r1[:, g], 1.0, 1.0, ALU.mult, ALU.add)
                me.link(pool.tensor_scalar(rtmp[:, g], mv1[:, g, 0], -1.0, 0.0, ALU.mult, ALU.add))
                pool.tensor_tensor(rtmp[:, g], rtmp[:, g], r1[:, g], ALU.mult).then_inc(x1_rstd, 1)

            def x12_step(p, b):
                wait(pool, stored[b], 16 * p)
                carry(pool)
                pool.wait_ge(x1_rstd, 2 * p + b + 1)
                carry(pool)
                for t in range(T):
                    g = b * T + t
                    ins = pool.tensor_scalar(x12[:, g], x1[:, g], rp1[:, g:g + 1], rtmp[:, g:g + 1], ALU.mult, ALU.add)
                me.link(ins)
                g = slice(b * T, (b + 1) * T)
                pool.wait_ge(consts_in, N_CONST)
                pool.tensor_tensor(x12[:, g], x12[:, g], o_bias[:], ALU.add).then_inc(x12_ready, 1)

            def pn(p, b, s):
                pool.wait_ge(inv_ready, 8 * p + 4 * b + s + 1)
                carry(pool)
                for u in range(2):
                    ins = pool.tensor_scalar(prob[:, b, s, u], prob[:, b, s, u], p_inv[:, b, s, u:u + 1], 1.0, ALU.mult, ALU.mult)
                ins.then_inc(prob_ready, 1)

            me.walk(dict(xs=xs, xq=xq_step, tail_a=tail_a, tail_b=tail_b, x12=x12_step, pn=pn))

        @block.vector
        def _(dve):
            me = Engine(dve, "vector")
            dve.wait_ge(zeros_made, 2)
            for tile in (n0[TE:P, :, 3 * TE:S], a0[TE:P, :, 3 * TE:S], q0[:], q1[:], q23[:], gate_w[:]):
                last = dve.memset(tile, 0.0)
            dve.memset(g_part[:].bitcast(F32), 0.0)
            last = dve.memset(a1[0:1, 0, 0:1], 0.0)
            last.then_inc(consts_ready, 1)
            dve.wait_ge(consts_in, N_CONST)
            dve.wait_ge(consts_ready, 1)
            dve.wait_ge(ident_made, 17)
            dve.tensor_copy(neg_sel[:], neg_sel0)
            dve.tensor_copy(mask[:], mask0)
            dve.tensor_copy(ident_r[:], ident[:])
            for k, col in ((0, 0), (1, NH)):
                dve.tensor_copy(gate_w[:, 0:C, col:col + NH], gate_raw[:, k, 0:C])
                dve.tensor_tensor(gate_w[:, C:2 * C, col:col + NH], gate_raw[:, k, C:2 * C], gate_raw[:, k, 2 * C:3 * C], ALU.add)
            dve.tensor_scalar(qb_s[:], qb[:], ATT_SCALE, None, ALU.mult).then_inc(consts_ready, 1)

            def xs(p, b):
                dve.wait_ge(x_loaded, 16 * p + 16)
                wait(dve, xq_ready, 2 * p - 1 + b)
                for g in (b * T, b * T + 1):
                    ins = dve.bn_stats(stat[:, g], x_in[:, g])
                me.link(ins, alone=True)
                for g in (b * T, b * T + 1):
                    ins = dve.bn_aggr(mv[:, g], stat[:, g])
                ins.then_inc(x_var, 1)

            def gsum(p):
                me.bank_filled()
                me.gates = me.bank

            def scan(p):
                dve.wait_ge(ln_ready, p + 1)
                me.link(dve.tensor_scalar(fg[:], me.gates[F_ROW:F_ROW + NH], gate_b[F_ROW:F_ROW + NH], 0.0, ALU.add, ALU.min))
                me.link(dve.tensor_tensor(fg[:], fg[:], ltmp, ALU.subtract))
                for b in range(PB):
                    w = slice(b * S, (b + 1) * S)
                    ins = dve.tensor_tensor_scan(cs[:, w], ones_row[:], fg[:, w], 0.0, ALU.mult, ALU.add)
                me.link(ins)
                wait(dve, dec_ready, 8 * p)
                me.link(dve.scalar_tensor_tensor(out=g_rows[0:NH], in0=me.gates[0:NH], scalar=gate_b[0:NH], in1=cs[:], op0=ALU.add, op1=ALU.subtract))
                for b in range(PB):
                    w = slice(b * S, (b + 1) * S)
                    ins = dve.tensor_tensor_scan(g_max[:, w], g_rows[0:NH, w], g_rows[0:NH, w], -3.0e38, ALU.max, ALU.max)
                me.link(ins)
                me.link(dve.tensor_copy(g_part[0:NH], g_max[:]))
                dve.tensor_tensor(g_part[F_ROW:F_ROW + NH], g_max[:], g_part[0:NH].bitcast(F32), ALU.subtract)
                dve.tensor_tensor(g_rows[F_ROW:F_ROW + NH], cs[:], g_max[:], ALU.add).then_inc(rows_ready, 1)

            def sx(p, b, h):
                me.bank_filled()
                dve.wait_ge(dec_ready, 8 * p + 4 * b + h + 1)
                wait(dve, u_ready, 8 * p + 4 * b + h - 3)
                dve.scalar_tensor_tensor(out=cmat[:, h].rearrange("p a b -> p (a b)"), in0=me.bank[:, 0:3 * P], scalar=QK_SCALE,
                                         in1=dec[:, h].rearrange("p a b -> p (a b)"), op0=ALU.mult, op1=ALU.mult).then_inc(c_ready, 1)

            def tail_a(p, b):
                dve.wait_ge(u_ready, 8 * p + 4 * b + 4)
                n = T * NH
                for t in range(T):
                    for h in range(NH):
                        ins = dve.bn_stats(ustat[:, b * n + t * NH + h], um[:, b * T + t, h, 0:DH])
                s = um[:, b * T:(b + 1) * T, :, DH:DH + 1].rearrange("p t h o -> p (t h o)")
                un, ut = unorm[:, b], utmp[:, b]
                me.link(dve.tensor_copy(ut, s))
                me.link(dve.scalar_tensor_tensor(out=un, in0=ut, scalar=-1.0, in1=ut, op0=ALU.mult, op1=ALU.max))
                dve.wait_ge(cols_ready, 2 * p + b + 1)
                me.link(dve.tensor_tensor(un, un, e_col[:, b * T:(b + 1) * T].rearrange("p t h -> p (t h)"), ALU.max))
                me.link(dve.tensor_scalar(un, un, EPS_GATE, None, ALU.add))
                me.link(dve.scalar_tensor_tensor(out=ut, in0=un, scalar=EPS_HEAD, in1=un, op0=ALU.mult, op1=ALU.mult), alone=True)
                for k in range(n):
                    ins = dve.bn_aggr(umv[:, b * n + k], ustat[:, b * n + k])
                me.link(ins)
                dve.tensor_tensor(uvar[:, b], ut, umv[:, b * n:(b + 1) * n, 1], ALU.add).then_inc(u_var, 1)

            def tail_b(p, b):
                n = T * NH
                dve.wait_ge(u_rstd, 2 * p + b + 1)
                wait(dve, x12_ready, 2 * p - 1 + b)
                for t in range(T):
                    for h in range(NH):
                        k = t * NH + h
                        ins = dve.tensor_scalar(x1[:, b * T + t, h * DH:(h + 1) * DH], um[:, b * T + t, h, 0:DH],
                                                umv[:, b * n + k, 0:1], urstd[:, b, k:k + 1], ALU.subtract, ALU.mult)
                me.link(ins)
                for g in (b * T, b * T + 1):
                    ins = dve.tensor_tensor(x1[:, g], x1[:, g], on_row[:], ALU.mult)
                me.link(ins)
                dve.wait_ge(xres_loaded, 16 * p + 16)
                g = slice(b * T, (b + 1) * T)
                me.link(dve.tensor_tensor(x1[:, g], x1[:, g], x_res[:, g], ALU.add))
                for g in (b * T, b * T + 1):
                    ins = dve.bn_stats(stat1[:, g], x1[:, g])
                me.link(ins, alone=True)
                for g in (b * T, b * T + 1):
                    ins = dve.bn_aggr(mv1[:, g], stat1[:, g])
                ins.then_inc(x1_ready, 1)

            def tail_c(p, b):
                dve.wait_ge(x1_rstd, 2 * p + b + 1)
                wait(dve, n_ready, 2 * p)
                for g in (b * T, b * T + 1):
                    ins = dve.tensor_scalar(xn[:, g], x1[:, g], mv1[:, g, 0:1], r2[:, g:g + 1], ALU.subtract, ALU.mult)
                ins.then_inc(xn_ready, 1)

            def s_step(p, b, s):
                me.bank_filled()
                dve.tensor_reduce(neg_max[:, b, s], me.bank[:].rearrange("p (u k) -> p u k", u=2), AX.X, ALU.max,
                                  negate=True).then_inc(max_ready, 1)

            def pn(p, b, s):
                dve.wait_ge(exp_done, 8 * p + 4 * b + s + 1)
                dve.reciprocal(p_inv[:, b, s], p_sum[:, b, s]).then_inc(inv_ready, 1)

            def o(p, k):
                me.bank_filled()
                if k == 0:
                    dve.wait_ge(x12_ready, 2 * p + 2)
                for b in range(PB):
                    dst = x12[k * TE:(k + 1) * TE, b * T, 0:D >> k]
                    ins = dve.tensor_tensor(dst, dst, me.bank[b * TE:(b + 1) * TE, 0:D >> k], ALU.add)
                if k == 1:
                    for e in range(2):
                        w = P >> e
                        dst = x12[e * TE:(e + 1) * TE, 1:PB * T:T, 0:w]
                        ins = dve.tensor_tensor(dst, dst, me.bank[e * TE:(e + 1) * TE, S:S + PB * P].rearrange("p (b n) -> p b n", b=PB)[:, :, 0:w], ALU.add)
                ins.then_inc(o_added, 1)

            me.walk(dict(xs=xs, gsum=gsum, scan=scan, sx=sx, tail_a=tail_a, tail_b=tail_b, tail_c=tail_c,
                         s=s_step, pn=pn, o=o))

        @block.scalar
        def _(act):
            me = Engine(act, "scalar")

            def copy(dst, src):
                return act.activation(dst, src, ACT.Copy)

            def add(dst, src, bias, scale=1.0):
                return act.activation(dst, src, ACT.Identity, bias=bias, scale=scale)

            def xt(p, b, cc):
                me.bank_filled()
                wait(act, c_ready, 8 * p)
                copy(xq_t[:, 2 * cc:2 * cc + 2, b], me.bank[:].rearrange("p (c i) -> p c i", c=2)).then_inc(xqt_ready, 1)

            def gsum(p):
                me.bank_filled()
                me.link(act.activation(ltmp, me.bank[F_ROW:F_ROW + NH], ACT.Abs, bias=gate_b[F_ROW:F_ROW + NH]))

            def lsg(p):
                me.link(act.activation(ltmp, ltmp, ACT.Exp, scale=-1.0))
                act.activation(ltmp, ltmp, ACT.Ln, bias=1.0).then_inc(ln_ready, 1)

            def cols(p, b):
                me.bank_filled()
                wait(act, x1_ready, 2 * p - 1 + b)
                g = slice(b * T, (b + 1) * T)
                v = me.bank[:, 0:T * P].rearrange("p (t r) -> p t r", t=T)
                copy(g_col[:, g], v[:, :, 0:NH])
                act.activation(e_col[:, g], v[:, :, F_ROW:F_ROW + NH], ACT.Exp, scale=-1.0).then_inc(cols_ready, 1)

            def marg(p, b, h):
                me.bank_filled()
                act.wait_ge(cols_ready, 2 * p + b + 1)
                wait(act, c_ready, 8 * p + 4 * b + h - 3)
                v = me.bank[:, 0:3 * P].rearrange("p (n q) -> p n q", n=3)
                act.activation(dec[:, h, 0:3:2], v[:, 0:3:2], ACT.Exp, bias=g_col[:, b * T, h:h + 1])
                act.activation(dec[:, h, 1], v[:, 1], ACT.Exp, bias=g_col[:, b * T + 1, h:h + 1]).then_inc(dec_ready, 1)

            def u(p, b, h):
                me.bank_filled()
                if h == 0:
                    wait(act, x1_ready, 2 * p - 1 + b)
                v = me.bank[:].rearrange("p (t n) -> p t n", t=T)[:, :, 0:DH + 1]
                copy(um[:, b * T:(b + 1) * T, h], v).then_inc(u_ready, 1)

            def nt(p, k):
                me.bank_filled()
                wait(act, v_ready, 4 * p)
                if k == 0:
                    v = me.bank[:].rearrange("p (b i) -> p b i", b=PB)
                    add(n0[0:TE], v[0:TE], nb[0:TE, 0:1], nw[0:TE, 0:1])
                    add(n0[TE:P, :, 0:3 * TE], v[TE:P, :, 0:3 * TE], nb[TE:P, 0:1], nw[TE:P, 0:1]).then_inc(n_ready, 1)
                else:
                    add(n1[:].rearrange("p b i -> p (b i)"), me.bank[:, 0:S], nb[:, 1:2], nw[:, 1:2])
                    for c in range(2):
                        ins = add(n2[:, c].rearrange("p b i -> p (b i)"), me.bank[:, S + c * P:S + (c + 1) * P], nb[:, 2 + c:3 + c], nw[:, 2 + c:3 + c])
                    ins.then_inc(n_ready, 1)

            def k_step(p, c):
                me.bank_filled()
                add(kt[:, c].rearrange("p b i -> p (b i)"), me.bank[:], kb[:, c:c + 1]).then_inc(k_ready, 1)

            def q0_step(p):
                me.bank_filled()
                for k in range(2):
                    rows = slice(k * FH, (k + 1) * FH)
                    ins = add(q0[rows, k].rearrange("p b i -> p (b i)"), me.bank[rows], qb_s[rows, 0:1], ATT_SCALE)
                ins.then_inc(q_ready, 1)

            def q1_step(p):
                me.bank_filled()
                for k in range(2):
                    rows = slice(k * FH, (k + 1) * FH)
                    add(q1[rows, k].rearrange("p b i -> p (b i)"), me.bank[rows, 0:S], qb_s[rows, 1:2], ATT_SCALE)
                for c in range(2):
                    v = me.bank[:, S + c * P:S + (c + 1) * P].rearrange("p (b i) -> p b i", b=PB)
                    for k in range(2):
                        rows = slice(k * FH, (k + 1) * FH)
                        ins = add(q23[rows, c, :, k], v[rows], qb_s[rows, 2 + c:3 + c], ATT_SCALE)
                ins.then_inc(q_ready, 1)

            def v_step(p, k):
                me.bank_filled()
                if k < 2:
                    for b in range(PB):
                        ins = copy(vf[k * TE:(k + 1) * TE, b * T], me.bank[b * TE:(b + 1) * TE])
                else:
                    ins = copy(vf[:, (k - 2) * T + 1], me.bank[:])
                ins.then_inc(v_ready, 1)

            def gate(p):
                me.bank_filled()
                wait(act, rows_ready, p)
                copy(gate_part[:], me.bank[:]).then_inc(gpart_ready, 1)

            def s_step(p, b, s):
                act.wait_ge(max_ready, 8 * p + 4 * b + s + 1)
                for k in range(2):
                    ins = act.activation(prob[:, b, s, k], me.bank[:, k * S:(k + 1) * S], ACT.Exp, bias=neg_max[:, b, s, k:k + 1],
                                         accum_out=p_sum[:, b, s, k:k + 1])
                ins.then_inc(exp_done, 1)

            def pt(p, b, s):
                me.bank_filled()
                copy(prob_t[:, b, :, s].rearrange("p k u q -> p k (u q)"), me.bank[:].rearrange("p (k n) -> p k n", k=T)).then_inc(probt_ready, 1)

            def pv0(p, b):
                me.bank_filled()
                wait(act, o_added, 2 * p)
                add(a0[:, b, 0:3 * TE], me.bank[:, 0:3 * TE], vb[:, 0:1])
                add(a0[0:TE, b, 3 * TE:S], me.bank[0:TE, 3 * TE:S], vb[0:TE, 0:1]).then_inc(a_ready, 1)

            def pv1(p, b):
                me.bank_filled()
                add(a1[:, b], me.bank[:, 0:P], vb[:, 1:2])
                for c in range(2):
                    n = P + c * TE
                    ins = add(a23[:, b, c], me.bank[:, n:n + TE], vb[:, 2 + c:3 + c])
                ins.then_inc(a_ready, 1)

            act.wait_ge(consts_in, N_CONST)
            act.wait_ge(consts_ready, 2)
            act.wait_ge(zeros_made, 2)
            me.walk(dict(xt=xt, gate=gate, gsum=gsum, lsg=lsg, cols=cols, marg=marg, u=u, nt=nt, k=k_step, q0=q0_step, q1=q1_step, v=v_step,
                         s=s_step, pt=pt, pv0=pv0, pv1=pv1))

        @block.tensor
        def _(pe):
            me = Engine(pe, "tensor")

            def mm(dst, lhs, rhs, first, last):
                return pe.matmul(dst, lhs, rhs, start=first, stop=last)

            def xt(p, b, cc):
                me.bank_free()
                pe.wait_ge(xq_ready, 2 * p + b + 1)
                for c in range(2):
                    for t in range(T):
                        n = (c * T + t) * P
                        f = (2 * cc + c) * P
                        ins = pe.transpose(me.bank[:, n:n + P], x_in[:, b * T + t, f:f + P], ident[:])
                ins.then_inc(me.ring.filled, 1)

            def gate(p):
                me.bank_free()
                pe.wait_ge(xqt_ready, 4 * p + 4)
                pe.wait_ge(kx_loaded, 16 * p + 16)
                for c in range(C):
                    mm(me.bank[c * GT:(c + 1) * GT], gate_w[:, c], xq_t[:, c].rearrange("p b i -> p (b i)"), True, False)
                for c in range(C):
                    dst = me.bank[c * GT:(c + 1) * GT].rearrange("p (b i) -> p b i", b=PB)
                    ins = mm(dst, gate_w[:, C + c], kx_t[:, c:PB * C:C], False, True)
                ins.then_inc(me.ring.filled, 1)

            def gsum(p):
                me.bank_free()
                pe.wait_ge(gpart_ready, p + 1)
                mm(me.bank[0:F_ROW + NH], gate_sel[:], gate_part[:], True, True).then_inc(me.ring.filled, 1)

            def cols(p, b):
                me.bank_free()
                pe.wait_ge(rows_ready, p + 1)
                for t in range(T):
                    w = slice((b * T + t) * P, (b * T + t + 1) * P)
                    ins = pe.transpose(me.bank[:, t * P:(t + 1) * P], g_rows[:, w], ident[:])
                ins.then_inc(me.ring.filled, 1)

            def marg(p, b, h):
                me.bank_free()
                pe.wait_ge(rows_ready, p + 1)
                mm(me.bank[:, 0:S], neg_sel[:, h], g_part[:, b * S:(b + 1) * S], True, False)
                mm(me.bank[:, 0:S], ident_r[:], mask[:].rearrange("p n q -> p (n q)"), False, True)
                mm(me.bank[:, S:S + P], neg_sel[:, h], g_part[:, b * S + P:(b + 1) * S], True, True).then_inc(me.ring.filled, 1)

            def sx(p, b, h):
                me.bank_free()
                k = kx_t[:, b * C + h]
                mm(me.bank[:, 0:4 * P].rearrange("p (n i) -> p n i", n=2)[:, :, 0:P], k[:, 0:P], xq_t[:, h, b].rearrange("p (t i) -> p t i", t=T), True, True)
                mm(me.bank[:, P:2 * P], k[:, P:S], xq_t[:, h, b, P:S], True, True).then_inc(me.ring.filled, 1)

            def u(p, b, h):
                me.bank_free()
                pe.wait_ge(c_ready, 8 * p + 4 * b + h + 1)
                pe.wait_ge(vx_loaded, 64 * p + 64)
                v0, v1 = vx[:, b * T, h], vx[:, b * T + 1, h]
                mm(me.bank[:, 0:DH + 1], cmat[:, h, 0], v0, True, True)
                mm(me.bank[:, S:S + DH + 1], cmat[:, h, 2], v0, True, False)
                mm(me.bank[:, S:S + DH + 1], cmat[:, h, 1], v1, False, True).then_inc(me.ring.filled, 1)

            def nt(p, k):
                me.bank_free()
                pe.wait_ge(xn_ready, 2 * p + 2)
                for b in range(PB):
                    if k == 0:
                        for t in range(T):
                            n = (b * T + t) * P
                            ins = pe.transpose(me.bank[:, n:n + P], xn[:, b * T + t, 0:P], ident[:])
                    else:
                        ins = pe.transpose(me.bank[:, b * P:(b + 1) * P], xn[:, b * T, P:2 * P], ident[:])
                        for c in range(2):
                            n = S + c * P + b * TE
                            ins = pe.transpose(me.bank[:, n:n + TE], xn[0:TE, b * T, (2 + c) * P:(3 + c) * P], ident[0:TE, 0:TE])
                ins.then_inc(me.ring.filled, 1)

            def project(dst, w, c, tokens):
                cols = slice(c * P, (c + 1) * P)
                inputs = [n0, n1, n2[:, 0], n2[:, 1]]
                for k in reversed(range(C)):
                    seen = min(tokens, (S, 2 * TE, TE, TE)[k])
                    src = inputs[k][:, :, 0:seen]
                    ins = pe.matmul(dst[:, :, 0:seen], w[:, k, cols], src, start=k == C - 1, stop=k == 0, skip_group_check=True)
                return ins

            def weights_loaded(p):
                if isinstance(p, int) and p == 0:
                    pe.wait_ge(weights_in, 64)

            def k_step(p, c):
                me.bank_free()
                pe.wait_ge(n_ready, 2 * p + 2)
                weights_loaded(p)
                project(me.bank[:].rearrange("p (b i) -> p b i", b=PB), wk, c, S).then_inc(me.ring.filled, 1)

            def q0_step(p):
                me.bank_free()
                pe.wait_ge(n_ready, 2 * p + 2)
                weights_loaded(p)
                project(me.bank[:].rearrange("p (b i) -> p b i", b=PB), wq, 0, S).then_inc(me.ring.filled, 1)

            def q1_step(p):
                me.bank_free()
                pe.wait_ge(n_ready, 2 * p + 2)
                weights_loaded(p)
                project(me.bank[:, 0:S].rearrange("p (b i) -> p b i", b=PB), wq, 1, 2 * TE)
                for c in range(2):
                    ins = project(me.bank[:, S + c * P:S + (c + 1) * P].rearrange("p (b i) -> p b i", b=PB), wq, 2 + c, TE)
                ins.then_inc(me.ring.filled, 1)

            def pair_of_batches(dst, inputs, w, n):
                for c, tokens in enumerate(inputs):
                    for b in range(PB):
                        ins = mm(dst[b * TE:(b + 1) * TE], tokens[:, b], w[:, c, 0:n], c == 0, c == len(inputs) - 1)
                return ins

            def v_step(p, k):
                me.bank_free()
                pe.wait_ge(n_ready, 2 * p + 2)
                weights_loaded(p)
                if k >= 2:
                    ins = mm(me.bank[:], n0[:, k - 2, P:S], wv[:, 0], True, True)
                else:
                    w = slice(k * TE, (k + 1) * TE)
                    tokens = [n0[:, :, w], n1[:, :, w], n2[:, 0], n2[:, 1]][0:C >> k]
                    ins = pair_of_batches(me.bank[:], tokens, wv, D)
                ins.then_inc(me.ring.filled, 1)

            def s_step(p, b, s):
                me.bank_free()
                pe.wait_ge(q_ready, 2 * p + 2)
                pe.wait_ge(k_ready, 4 * p + 4)
                for u in range(2):
                    dst = me.bank[:, u * S:(u + 1) * S]
                    if s < 2:
                        ins = mm(dst, q0[:, u, b, s * P:(s + 1) * P], kt[:, 0, b], True, True)
                    elif s == 2:
                        ins = mm(dst, q1[:, u, b], kt[:, 1, b], True, True)
                    else:
                        ins = mm(dst, q23[:, u, b].rearrange("p k i -> p (k i)"), kt[:, 2 + u, b], True, True)
                ins.then_inc(me.ring.filled, 1)

            def pt(p, b, s):
                me.bank_free()
                pe.wait_ge(prob_ready, 8 * p + 4 * b + s + 1)
                for k in range(T):
                    for u in range(2):
                        n = (k * 2 + u) * P
                        ins = pe.transpose(me.bank[:, n:n + P], prob[:, b, s, u, k * P:(k + 1) * P], ident[:])
                ins.then_inc(me.ring.filled, 1)

            def pair_of_heads(dst, b, c, probs):
                for k in range(T):
                    for u in range(2):
                        f = c * P + u * FH
                        ins = mm(dst[u * FH:(u + 1) * FH], vf[:, b * T + k, f:f + FH], probs(k, u), k == 0, k == T - 1)
                return ins

            def pv0(p, b):
                me.bank_free()
                pe.wait_ge(probt_ready, 8 * p + 4 * b + 2)
                pe.wait_ge(v_ready, 4 * p + 4)
                pair_of_heads(me.bank[:, 0:S].rearrange("p (s q) -> p s q", s=2), b, 0,
                              lambda k, u: prob_t[:, b, k, 0:2, u]).then_inc(me.ring.filled, 1)

            def pv1(p, b):
                me.bank_free()
                pe.wait_ge(probt_ready, 8 * p + 4 * b + 4)
                pair_of_heads(me.bank[:, 0:P], b, 1, lambda k, u: prob_t[:, b, k, 2, u])
                for c in range(2):
                    n = P + c * TE
                    ins = pair_of_heads(me.bank[:, n:n + TE], b, 2 + c, lambda k, u: prob_t[:, b, k, 3, c, u * TE:(u + 1) * TE])
                ins.then_inc(me.ring.filled, 1)

            def o(p, k):
                me.bank_free()
                pe.wait_ge(a_ready, 4 * p + 4)
                w = slice(k * TE, (k + 1) * TE)
                inputs = [a0[:, :, w], a1[:, :, w], a23[:, :, 0], a23[:, :, 1]][0:C >> k]
                ins = pair_of_batches(me.bank[:, 0:D >> k], inputs, wo, D >> k)
                if k == 1:
                    for b in range(PB):
                        ins = mm(me.bank[:, S + b * P:S + (b + 1) * P], a0[:, b, P:S], wo[:, 0, 0:P], True, True)
                ins.then_inc(me.ring.filled, 1)

            pe.wait_ge(ident_made, 17)
            pe.wait_ge(zeros_made, 2)
            pe.wait_ge(consts_ready, 2)
            me.walk(dict(xt=xt, gate=gate, gsum=gsum, cols=cols, marg=marg, sx=sx, u=u, nt=nt, k=k_step, q0=q0_step, q1=q1_step, v=v_step,
                         s=s_step, pt=pt, pv0=pv0, pv1=pv1, o=o))


_OUT = ((B, S, D), "float32")


def kernel(**inputs):
    import numpy as np
    import concourse.bacc as bacc
    from concourse.bass_utils import run_bass_kernel_spmd as run

    def get(name):
        return np.asarray(inputs[name])

    def column(name):
        return get(name).reshape(C, P).T

    laid = {
        "x": get("x"), "ctx": get("ctx_1024"), "ctx_t": get("ctx_1024").transpose(0, 2, 1),
        "ig_w": get("L0_xattn_igate_kernel"), "ig_b": get("L0_xattn_igate_bias").reshape(NH, 1),
        "fg_w": get("L0_xattn_fgate_kernel"), "fg_b": get("L0_xattn_fgate_bias").reshape(NH, 1),
        "on_scale": get("L0_xattn_outnorm_scale").reshape(1, D),
        "n_w": column("L0_ffn_norm_w"), "n_b": column("L0_ffn_norm_b"),
        "wq_t": get("L0_ffn_q_w").T, "q_b": column("L0_ffn_q_b"), "wk_t": get("L0_ffn_k_w").T, "k_b": column("L0_ffn_k_b"),
        "wv_t": get("L0_ffn_v_w").T, "v_b": column("L0_ffn_v_b"), "wo_t": get("L0_ffn_o_w").T,
        "o_b": get("L0_ffn_o_b").reshape(1, D),
    }
    nc = bacc.Bacc("TRN2", target_bir_lowering=False, num_devices=1)
    arrays, args = {}, []
    for name, a in laid.items():
        arrays[f"in_{name}"] = np.ascontiguousarray(a)
        args.append(nc.dram_tensor(f"in_{name}", a.shape, mybir.dt.from_np(a.dtype), kind="ExternalInput").ap())
    args.append(nc.dram_tensor("out_0", _OUT[0], F32, kind="ExternalOutput").ap())
    xattn_ffn(nc, *args)
    r = run(nc, [arrays], core_ids=[0])
    return r.results[0]["out_0"]
```

```python
from contextlib import ExitStack

import concourse.bass as bass
from concourse import mybir

F32 = mybir.dt.float32
F32R = mybir.dt.float32r
ALU = mybir.AluOpType
ACT = mybir.ActivationFunctionType
AX = mybir.AxisListType

B, S, D = 16, 256, 512
P = 128
PB = 2
PAIRS = B // PB
T = S // P
C = D // P
NH, DH = 4, 128
E = 4
TE = S // E
FH = D // 8
EPS_X, EPS_GATE, EPS_HEAD, EPS_FFN = 1e-5, 1e-6, 1e-6, 1e-5
QK_SCALE = DH ** -0.5
ATT_SCALE = D ** -0.5
SPARE = 16
MASKED = -2.0 ** 100
GT = 32
F_ROW = 32

BODY = [
    ("F", "x12", 0), ("F", "nt", 0), ("T", "tail_a", 0), ("G", "xs", 0), ("T", "tail_a", 1), ("F", "nt", 1),
    ("T", "norm", 0, 0), ("F", "x12", 1), ("F", "v", 0), ("F", "v", 1), ("F", "k", 0), ("F", "k", 1), ("F", "k", 2),
    ("F", "k", 3), ("T", "norm", 0, 1), ("F", "q0"), ("F", "q1"), ("F", "v", 2), ("X", "cols", 0), ("T", "res", 0, 0),
    ("T", "res", 0, 1), ("T", "tail_b", 0), ("F", "s", 0, 0), ("F", "s", 0, 1), ("T", "norm", 1, 0),
    ("F", "pn", 0, 0), ("F", "v", 3), ("T", "norm", 1, 1), ("X", "marg", 0, 0), ("F", "s", 0, 2), ("F", "s", 0, 3),
    ("F", "pn", 0, 1), ("X", "sx", 0, 0), ("T", "res", 1, 0), ("F", "pn", 0, 2), ("F", "pn", 0, 3),
    ("X", "marg", 0, 1), ("F", "pt", 0, 0), ("X", "marg", 0, 2), ("F", "s", 1, 0), ("F", "s", 1, 1),
    ("X", "sx", 0, 1), ("T", "res", 1, 1), ("F", "pt", 0, 1), ("X", "marg", 0, 3), ("F", "pt", 0, 2),
    ("F", "s", 1, 2), ("F", "pn", 1, 0), ("F", "s", 1, 3), ("X", "sx", 0, 2), ("X", "sx", 0, 3), ("X", "u", 0, 0),
    ("F", "pt", 0, 3), ("X", "cols", 1), ("F", "pn", 1, 1), ("F", "pn", 1, 2), ("X", "marg", 1, 0), ("F", "pn", 1, 3),
    ("T", "tail_b", 1), ("T", "tail_c", 0), ("X", "u", 0, 1), ("F", "pv0", 0), ("X", "ustat", 0, 0),
    ("X", "sx", 1, 0), ("X", "marg", 1, 1), ("G", "xs", 1), ("X", "u", 0, 2), ("X", "ustat", 0, 1), ("G", "xq", 0),
    ("X", "marg", 1, 2), ("F", "pt", 1, 0), ("X", "marg", 1, 3), ("X", "ustat", 0, 2), ("X", "u", 0, 3),
    ("X", "sx", 1, 1), ("X", "ustat", 0, 3), ("F", "pt", 1, 1), ("X", "sx", 1, 2), ("X", "sx", 1, 3), ("F", "pv1", 0),
    ("F", "pt", 1, 2), ("F", "pt", 1, 3), ("F", "pv0", 1), ("G", "xq", 1), ("X", "ustat", 1, 0), ("G", "xt", 0, 0),
    ("X", "u", 1, 0), ("G", "xt", 0, 1), ("G", "xt", 1, 0), ("X", "u", 1, 1), ("G", "xt", 1, 1), ("T", "tail_c", 1),
    ("F", "pv1", 1), ("G", "gate"), ("X", "ustat", 1, 1), ("X", "u", 1, 2), ("X", "u", 1, 3), ("G", "gsum"),
    ("X", "ustat", 1, 2), ("G", "lsg"), ("F", "o", 0), ("F", "o", 1), ("G", "scan_f"), ("G", "scan"),
    ("X", "ustat", 1, 3),
]
LAG = {"F": 0, "T": 1, "X": 2, "G": 3}
SPANS = {
    ("G", 0): (8, 21), ("X", 0): (87, 110), ("T", 0): (104, 182), ("G", 1): (88, 153), ("X", 1): (164, 173), ("G", 2): (167, 179),
}


def spread():
    placed = []
    for (stage, pair), (start, end) in SPANS.items():
        steps = [s for s in BODY if s[0] == stage]
        placed += [(start * 1000 + (end - start) * 1000 * k // len(steps), s, pair - LAG[stage]) for k, s in enumerate(steps)]
    return [(s, turn) for _, s, turn in sorted(placed, key=lambda x: x[0])]


ORDER = {
    "fill": spread(),
    "body": [(s, 0) for s in BODY],
    "drain1": [(s, 0) for s in BODY if s[0] in "FTX"],
    "drain2": [(s, 0) for s in BODY if s[0] in "FT"],
    "drain3": [(s, 0) for s in BODY if s[0] == "F"],
}
ROUND = {"fill": 0, "drain1": PAIRS - 3, "drain2": PAIRS - 2, "drain3": PAIRS - 1}

RING_OF = {
    "nt": "turn", "xt": "turn", "pt": "turn",
    "k": "prod", "q0": "prod", "q1": "prod", "v": "prod", "pv0": "prod", "pv1": "prod", "o": "prod", "u": "prod",
    "s": "attn",
    "gate": "xatt", "gsum": "xatt", "cols": "xatt", "marg": "xatt", "sx": "xatt",
}
OWN = {"vector": {"G": 8, "X": 2, "T": 26, "F": 0}, "scalar": {"G": 2, "X": 0, "T": 0, "F": 0}, "gpsimd": {"G": 4, "X": 0, "T": 16, "F": 2}}


class Ring:

    def __init__(self, name, ctx, nc):
        self.banks = [ctx.enter_context(nc.psum_tensor(f"{name}{k}", [P, 512], F32)) for k in range(2)]
        self.filled = ctx.enter_context(nc.semaphore(f"{name}_filled"))
        self.jobs = {ph: [job for job in ORDER[ph] if RING_OF.get(job[0][1]) == name] for ph in ORDER}
        assert len(self.jobs["body"]) % 2 == 0

    def place(self, phase, i, job):
        n = 1 + self.jobs[phase].index(job)
        for ph in ORDER:
            if ph == phase:
                break
            if ph != "body":
                n += len(self.jobs[ph])
        bank = self.banks[(n - 1) % 2]
        if phase == "body":
            n = i * len(self.jobs["body"]) + n
        elif phase != "fill":
            n += (PAIRS - 3) * len(self.jobs["body"])
        return bank, n

    def before(self, phase, i, job):
        ago = 2
        n = self.jobs[phase].index(job)
        names = list(ORDER)
        while n < ago:
            ago -= n
            if phase == "fill":
                return None
            if phase != "body" or isinstance(i, int) and i == 0:
                phase = names[names.index(phase) - 1]
                i = PAIRS - 4 if phase == "body" else ROUND[phase]
            else:
                i = i - 1
            n = len(self.jobs[phase])
        step, turn = self.jobs[phase][n - ago]
        return step, i + turn + LAG[step[0]]


def xattn_ffn(nc, x, ctx_in, ctx_t, ig_w, ig_b, fg_w, fg_b, on_scale, n_w, n_b,
              wq_t, q_b, wk_t, k_b, wv_t, v_b, wo_t, o_b, out):
    ctx = ExitStack()
    with ctx:
        def sb(name, shape, dtype=F32):
            return ctx.enter_context(nc.sbuf_tensor(name, shape, dtype))

        def sem(name):
            return ctx.enter_context(nc.semaphore(name))

        rings = {n: Ring(n, ctx, nc) for n in ("turn", "prod", "attn", "xatt")}

        ident = sb("ident", [P, P])
        neg_sel = sb("neg_sel", [F_ROW + NH, NH, P], F32R)
        ident_r = sb("ident_r", [P, P], F32R)
        mask = sb("mask", [P, 2, P], F32R)
        wq, wk, wv, wo = (sb(n, [P, C, D]) for n in ("wq", "wk", "wv", "wo"))
        gate_raw = sb("gate_raw", [P, 2, 3 * C, NH])
        gate_w = sb("gate_w", [P, 2 * C, GT])
        gate_sel = sb("gate_sel", [P, F_ROW + NH])
        gate_part = sb("gate_part", [P, PB * S])
        gate_b = sb("gate_b", [F_ROW + NH, 1])
        on_row = sb("on_row", [P, D])
        o_bias = sb("o_bias", [P, T, D])
        qb, kb, vb, nw, nb = (sb(n, [P, C]) for n in ("qb", "kb", "vb", "nw", "nb"))
        qb_s = sb("qb_s", [P, C])
        pool_spare, dve_spare = sb("pool_spare", [1, SPARE + 1]), sb("dve_spare", [1, SPARE + 1])
        minus_half = sb("minus_half", [P, 8])
        ones_row = sb("ones_row", [NH, S])
        x_in = sb("x_in", [P, PB * T, D])
        x_res = sb("x_res", [P, PB * T, D])
        xn = sb("xn", [P, PB * T, D])
        xq_t = sb("xq_t", [P, C, PB, S])
        kx_t = sb("kx_t", [P, PB * C, S])
        vx = sb("vx", [P, PB * T, NH, DH + 1])
        stat = sb("stat", [P, PB * T, 6])
        mv = sb("mv", [P, PB * T, 2])
        rstd = sb("rstd", [P, PB * T])
        x_off = sb("x_off", [P, PB * T])
        fg = sb("fg", [NH, PB * S])
        ltmp = gate_part[0:NH]
        cs = sb("cs", [NH, PB * S])
        g_rows = sb("g_rows", [P, PB * S])
        g_max = sb("g_max", [NH, PB * S])
        g_part = sb("g_part", [F_ROW + NH, PB * S], F32R)
        g_col = sb("g_col", [P, PB * T, NH])
        e_col = sb("e_col", [P, PB * T, NH])
        dec = sb("dec", [P, NH, 3, P])
        neg_sel0 = dec[0:F_ROW + NH, :, 0]
        mask0 = dec[:, :, 1][:, 0:2]
        cmat = sb("cmat", [P, NH, 3, P])
        um = sb("um", [P, PB * T, NH, DH + 1])
        ustat = sb("ustat", [P, PB * T * NH, 6])
        umv = sb("umv", [P, PB * T * NH, 2])
        unorm = sb("unorm", [P, PB, T * NH])
        utmp = sb("utmp", [P, PB, T * NH])
        uvar = sb("uvar", [P, PB, T * NH])
        urstd = sb("urstd", [P, PB, T * NH])
        x1 = sb("x1", [P, PB * T, D])
        stat1 = sb("stat1", [P, PB * T, 6])
        mv1 = sb("mv1", [P, PB * T, 2])
        r1 = sb("r1", [P, PB * T])
        rp1 = sb("rp1", [P, PB * T])
        r2 = sb("r2", [P, PB * T])
        rtmp = sb("rtmp", [P, PB * T])
        n0 = sb("n0", [P, PB, S])
        n1 = sb("n1", [P, PB, 2 * TE])
        n2 = sb("n2", [P, 2, PB, TE])
        kt = sb("kt", [P, C, PB, S])
        q0 = sb("q0", [P, 2, PB, S])
        q1 = sb("q1", [P, 2, PB, 2 * TE])
        q23 = sb("q23", [P, 2, PB, 2, TE])
        vf = sb("vf", [P, PB * T, D])
        neg_max = sb("neg_max", [P, PB, 4, 2])
        p_sum = sb("p_sum", [P, PB, 4, 2])
        p_inv = sb("p_inv", [P, PB, 4, 2])
        prob = sb("prob", [P, PB, 4, 2, S])
        prob_t = sb("prob_t", [P, PB, T, 4, 2, P])
        a0 = sb("a0", [P, PB, S])
        a1 = sb("a1", [P, PB, 2 * TE])
        a23 = sb("a23", [P, PB, 2, TE])
        x12 = sb("x12", [P, PB * T, D])

        consts_in, weights_in = sem("consts_in"), sem("weights_in")
        ident_made = sem("ident_made")
        zeros_made = sem("zeros_made")
        consts_ready = sem("consts_ready")
        x_loaded, kx_loaded, vx_loaded, xres_loaded = (sem(n) for n in ("x_loaded", "kx_loaded", "vx_loaded", "xres_loaded"))
        stored = [sem(f"stored{b}") for b in range(PB)]
        x_var = sem("x_var")
        x_off_ready = sem("x_off_ready")
        xq_ready = sem("xq_ready")
        xqt_ready = sem("xqt_ready")
        gpart_ready = sem("gpart_ready")
        ln_ready = sem("ln_ready")
        rows_ready = sem("rows_ready")
        cols_ready = sem("cols_ready")
        dec_ready = sem("dec_ready")
        c_ready = sem("c_ready")
        u_ready = sem("u_ready")
        u_var = sem("u_var")
        u_rstd = sem("u_rstd")
        x1_ready = sem("x1_ready")
        x1_rstd = sem("x1_rstd")
        xn_ready = sem("xn_ready")
        n_ready = sem("n_ready")
        k_ready = sem("k_ready")
        q_ready = sem("q_ready")
        v_ready = sem("v_ready")
        max_ready = sem("max_ready")
        exp_done = sem("exp_done")
        inv_ready = sem("inv_ready")
        prob_ready = sem("prob_ready")
        probt_ready = sem("probt_ready")
        a_ready = sem("a_ready")
        x12_ready = sem("x12_ready")
        o_added = sem("o_added")
        own = {e: {s: sem(f"own_{e}_{s}") for s in LAG} for e in OWN}

        READ = {
            "xt": lambda b, cc: (xqt_ready, 4, 2 * b + cc + 1), "nt": lambda k: (n_ready, 2, k + 1),
            "pt": lambda b, s: (probt_ready, 8, 4 * b + s + 1),
            "k": lambda c: (k_ready, 4, c + 1), "q0": lambda: (q_ready, 2, 1), "q1": lambda: (q_ready, 2, 2),
            "v": lambda k: (v_ready, 4, k + 1), "o": lambda k: (o_added, 2, k + 1),
            "pv0": lambda b: (a_ready, 4, 2 * b + 1), "pv1": lambda b: (a_ready, 4, 2 * b + 2),
            "u": lambda b, h: (u_ready, 8, 4 * b + h + 1), "s": lambda b, s: (exp_done, 8, 4 * b + s + 1),
            "gate": lambda: (gpart_ready, 1, 1), "gsum": lambda: (rows_ready, 1, 1), "cols": lambda b: (cols_ready, 2, b + 1),
            "marg": lambda b, h: (dec_ready, 8, 4 * b + h + 1), "sx": lambda b, h: (c_ready, 8, 4 * b + h + 1),
        }

        def wait(eng, s, n):
            if not isinstance(n, int) or n > 0:
                eng.wait_ge(s, n)

        carried = [0]

        def carry(eng):
            carried[0] = k = carried[0] % SPARE + 1
            if eng.engine == nc.gpsimd.engine:
                eng.tensor_tensor(pool_spare[:, k:k + 1], pool_spare[:, 0:1], pool_spare[:, 0:1], ALU.mult)
            else:
                eng.tensor_copy(dve_spare[:, k:k + 1], dve_spare[:, 0:1])

        class Engine:

            def __init__(self, eng, name):
                self.eng, self.name = eng, name

            def link(self, ins, alone=False):
                s = own[self.name][self.stage]
                self.count[0] += 1
                ins.then_inc(s, 1)
                self.eng.wait_ge(s, self.p * OWN[self.name][self.stage] + self.count[0])
                if alone:
                    carry(self.eng)

            def run(self, steps, phase, i):
                counts = {}
                for step, turn in ORDER[phase]:
                    self.stage, what, *args = step
                    self.p = i + turn + LAG[self.stage]
                    self.count = counts.setdefault((self.stage, turn), [0])
                    if what in RING_OF:
                        self.ring = rings[RING_OF[what]]
                        self.bank, self.fills = self.ring.place(phase, i, (step, turn))
                        self.before = self.ring.before(phase, i, (step, turn))
                    if what in steps:
                        steps[what](self.p, *args)
                for (s, _), count in counts.items():
                    assert self.name not in OWN or count[0] == OWN[self.name][s], (self.name, s, count[0])

            def walk(self, steps):
                for phase in ORDER:
                    if phase != "body":
                        self.run(steps, phase, ROUND[phase])
                        continue
                    self.run(steps, "body", 0)
                    with self.eng.Fori(1, PAIRS - 3) as i:
                        self.run(steps, "body", i)

            def bank_filled(self):
                self.eng.wait_ge(self.ring.filled, self.fills)

            def bank_free(self):
                if self.before is not None:
                    (_, what, *args), pair = self.before
                    s, per_pair, n = READ[what](*args)
                    self.eng.wait_ge(s, pair * per_pair + n)

        x_d = x.rearrange("(p b) (t q) d -> p q (b t) d", b=PB, q=P)
        ctx_d = ctx_in.rearrange("(p b) (t q) d -> p q (b t) d", b=PB, q=P)
        ctxt_d = ctx_t.rearrange("(p b) (c q) i -> p q (b c) i", b=PB, q=P)
        out_d = out.rearrange("p (t q) d -> p q t d", q=P)

        block = ctx.enter_context(nc.Block())

        @block.sync
        def _(sp):
            def load_x(p):
                sp.dma_start(x_in[:], x_d[p]).then_inc(x_loaded, 16)

            def load_kx(p):
                sp.dma_start(kx_t[:], ctxt_d[p]).then_inc(kx_loaded, 16)

            def load_vx(p):
                for g in range(PB * T):
                    sp.dma_start(vx[:, g, :, 0:DH], ctx_d[p, :, g, :].rearrange("q (h d) -> q h d", h=NH)).then_inc(vx_loaded, 16)

            def load_xres(p):
                sp.dma_start(x_res[:], x_d[p]).then_inc(xres_loaded, 16)

            def store(p, b):
                sp.wait_ge(o_added, 2 * p + 2)
                sp.dma_start(out_d[p * PB + b], x12[:, b * T:(b + 1) * T, :]).then_inc(stored[b], 16)

            load_x(0)
            sp.wait_ge(zeros_made, 1)
            for n, (tile, w) in enumerate(((gate_raw[:, 0], ig_w), (gate_raw[:, 1], fg_w))):
                sp.dma_start(tile, w.rearrange("(c p) h -> p c h", p=P)).then_inc(consts_in, 16)
            sp.dma_start(gate_b[0:NH], ig_b).then_inc(consts_in, 16)
            sp.dma_start(gate_b[F_ROW:F_ROW + NH], fg_b).then_inc(consts_in, 16)
            for tile, v in ((qb, q_b), (kb, k_b), (vb, v_b), (nw, n_w), (nb, n_b)):
                sp.dma_start(tile[:], v).then_inc(consts_in, 16)
            sp.dma_start(on_row[:], on_scale.partition_broadcast(P)).then_inc(consts_in, 16)
            for e in range(E):
                rows = slice(TE * (e % 2), TE * (e % 2 + 1))
                sp.dma_start(o_bias[rows, e // 2, 0:D >> e], o_b[:, 0:D >> e].partition_broadcast(TE)).then_inc(consts_in, 16)
            load_kx(0)
            load_vx(0)
            load_xres(0)
            for tile, w in ((wk, wk_t), (wq, wq_t), (wv, wv_t), (wo, wo_t)):
                sp.dma_start(tile[:], w.rearrange("(c p) n -> p c n", p=P)).then_inc(weights_in, 16)

            def reload(p):
                sp.wait_ge(c_ready, 8 * p)
                load_kx(p)
                sp.wait_ge(u_ready, 8 * p)
                load_vx(p)

            def reload_x(p):
                sp.wait_ge(xqt_ready, 4 * p)
                load_x(p)

            def reload_xres(p):
                sp.wait_ge(x1_ready, 2 * p)
                load_xres(p)

            reload_x(1)
            reload(1)
            reload_x(2)
            reload_xres(1)
            reload(2)
            reload_x(3)
            with sp.Fori(0, PAIRS - 4) as i:
                reload_xres(i + 2)
                reload(i + 3)
                reload_x(i + 4)
                store(i, 0)
                store(i, 1)
            reload_xres(PAIRS - 2)
            reload(PAIRS - 1)
            store(PAIRS - 4, 0)
            store(PAIRS - 4, 1)
            reload_xres(PAIRS - 1)
            for p in range(PAIRS - 3, PAIRS):
                store(p, 0)
                store(p, 1)
            for b in range(PB):
                sp.wait_ge(stored[b], 16 * PAIRS)

        N_CONST = 16 * 14

        @block.gpsimd
        def _(pool):
            pool.memset(gate_b[:], 0.0)
            pool.memset(o_bias[:], 0.0).then_inc(zeros_made, 1)
            pool.memset(ident[:], 0.0).then_inc(ident_made, 1)
            pool.memset(neg_sel0, 0.0).then_inc(ident_made, 1)
            pool.memset(gate_sel[:], 0.0).then_inc(ident_made, 1)
            pool.memset(minus_half[:], -0.5).then_inc(ident_made, 1)
            pool.wait_ge(ident_made, 4)
            pool.affine_select(out=ident[:], in_=ident[:], compare_op=ALU.not_equal, fill=1.0, base=0,
                               pattern=[[-1, P]], channel_multiplier=1).then_inc(ident_made, 1)
            for k in range(2):
                pool.affine_select(out=neg_sel0, in_=neg_sel0, compare_op=ALU.not_equal, fill=-1.0, base=F_ROW * k,
                                   pattern=[[1, NH], [0, P]], channel_multiplier=-1).then_inc(ident_made, 1)
                pool.wait_ge(ident_made, 6 + k)
            n = 7
            for c in range(C):
                for k in range(2):
                    pool.affine_select(out=gate_sel[:, F_ROW * k:F_ROW * k + NH], in_=gate_sel[:, F_ROW * k:F_ROW * k + NH],
                                       compare_op=ALU.not_equal, fill=1.0, base=GT * c + NH * k,
                                       pattern=[[1, NH]], channel_multiplier=-1).then_inc(ident_made, 1)
                n += 2
                pool.wait_ge(ident_made, n)
            pool.memset(mask0, 0.0).then_inc(ident_made, 1)
            pool.wait_ge(ident_made, n + 1)
            pool.affine_select(out=mask0, in_=mask0, compare_op=ALU.is_ge, fill=MASKED, base=0,
                               pattern=[[0, 2], [1, P]], channel_multiplier=-1).then_inc(ident_made, 1)
            pool.memset(ones_row[:], 1.0)
            pool.memset(pool_spare[:], 1.0)
            pool.memset(vx[:, :, :, DH:DH + 1], 1.0)
            pool.memset(g_rows[:], 0.0).then_inc(zeros_made, 1)
            me = Engine(pool, "gpsimd")

            def rsqrt(dst, var, eps, n):
                me.link(pool.tensor_scalar(dst, var, 1.0, eps, ALU.mult, ALU.add))
                return pool.tensor_tensor(dst, dst, minus_half[:, 0:n], ALU.pow)

            def xs(p, b):
                g = slice(b * T, (b + 1) * T)
                pool.wait_ge(x_var, 2 * p + b + 1)
                carry(pool)
                pool.tensor_scalar(x_off[:, g], mv[:, g, 0], -1.0, 0.0, ALU.mult, ALU.add)
                me.link(rsqrt(rstd[:, g], mv[:, g, 1], EPS_X, T))
                pool.tensor_tensor(x_off[:, g], x_off[:, g], rstd[:, g], ALU.mult).then_inc(x_off_ready, 1)

            def xq_step(p, b):
                pool.wait_ge(x_off_ready, 2 * p + b + 1)
                carry(pool)
                for g in (b * T, b * T + 1):
                    ins = pool.tensor_scalar(x_in[:, g], x_in[:, g], rstd[:, g:g + 1], x_off[:, g:g + 1], ALU.mult, ALU.add)
                ins.then_inc(xq_ready, 1)

            def tail_a(p, b):
                pool.wait_ge(u_var, 2 * p + b + 1)
                carry(pool)
                pool.tensor_tensor(urstd[:, b], uvar[:, b], minus_half[:], ALU.pow).then_inc(u_rstd, 1)

            def tail_b(p, b):
                g = slice(b * T, (b + 1) * T)
                pool.wait_ge(x1_ready, 2 * p + b + 1)
                carry(pool)
                me.link(rsqrt(r1[:, g], mv1[:, g, 1], EPS_X, T))
                me.link(pool.tensor_tensor(rtmp[:, g], r1[:, g], r1[:, g], ALU.mult))
                me.link(pool.tensor_tensor(rtmp[:, g], rtmp[:, g], mv1[:, g, 1], ALU.mult), alone=True)
                me.link(rsqrt(r2[:, g], rtmp[:, g], EPS_FFN, T))
                me.link(pool.tensor_tensor(r2[:, g], r2[:, g], r1[:, g], ALU.mult), alone=True)
                pool.tensor_scalar(rp1[:, g], r1[:, g], 1.0, 1.0, ALU.mult, ALU.add)
                me.link(pool.tensor_scalar(rtmp[:, g], mv1[:, g, 0], -1.0, 0.0, ALU.mult, ALU.add))
                pool.tensor_tensor(rtmp[:, g], rtmp[:, g], r1[:, g], ALU.mult).then_inc(x1_rstd, 1)

            def x12_step(p, b):
                wait(pool, stored[b], 16 * p)
                carry(pool)
                pool.wait_ge(x1_rstd, 2 * p + b + 1)
                carry(pool)
                for t in range(T):
                    g = b * T + t
                    ins = pool.tensor_scalar(x12[:, g], x1[:, g], rp1[:, g:g + 1], rtmp[:, g:g + 1], ALU.mult, ALU.add)
                me.link(ins)
                g = slice(b * T, (b + 1) * T)
                pool.wait_ge(consts_in, N_CONST)
                pool.tensor_tensor(x12[:, g], x12[:, g], o_bias[:], ALU.add).then_inc(x12_ready, 1)

            def pn(p, b, s):
                pool.wait_ge(inv_ready, 8 * p + 4 * b + s + 1)
                carry(pool)
                for u in range(2):
                    ins = pool.tensor_scalar(prob[:, b, s, u], prob[:, b, s, u], p_inv[:, b, s, u:u + 1], 1.0, ALU.mult, ALU.mult)
                ins.then_inc(prob_ready, 1)

            me.walk(dict(xs=xs, xq=xq_step, tail_a=tail_a, tail_b=tail_b, x12=x12_step, pn=pn))

        @block.vector
        def _(dve):
            me = Engine(dve, "vector")
            for tile in (n0[TE:P, :, 3 * TE:S], a0[TE:P, :, 3 * TE:S], q0[:], q1[:], q23[:], gate_w[:]):
                dve.memset(tile, 0.0)
            dve.memset(dve_spare[:], 1.0)
            dve.memset(g_part[:].bitcast(F32), 0.0).then_inc(consts_ready, 1)
            dve.wait_ge(consts_in, N_CONST)
            dve.wait_ge(consts_ready, 1)
            dve.wait_ge(ident_made, 17)
            dve.tensor_copy(neg_sel[:], neg_sel0)
            dve.tensor_copy(mask[:], mask0)
            dve.tensor_copy(ident_r[:], ident[:])
            for k, col in ((0, 0), (1, NH)):
                dve.tensor_copy(gate_w[:, 0:C, col:col + NH], gate_raw[:, k, 0:C])
                dve.tensor_tensor(gate_w[:, C:2 * C, col:col + NH], gate_raw[:, k, C:2 * C], gate_raw[:, k, 2 * C:3 * C], ALU.add)
            dve.tensor_scalar(qb_s[:], qb[:], ATT_SCALE, None, ALU.mult).then_inc(consts_ready, 1)
            dve.wait_ge(zeros_made, 2)

            def xs(p, b):
                dve.wait_ge(x_loaded, 16 * p + 16)
                wait(dve, xq_ready, 2 * p - 1 + b)
                for g in (b * T, b * T + 1):
                    ins = dve.bn_stats(stat[:, g], x_in[:, g])
                me.link(ins, alone=True)
                for g in (b * T, b * T + 1):
                    ins = dve.bn_aggr(mv[:, g], stat[:, g])
                ins.then_inc(x_var, 1)

            def gsum(p):
                me.bank_filled()
                me.gates = me.bank

            def scan_f(p):
                dve.wait_ge(ln_ready, p + 1)
                me.link(dve.tensor_scalar(fg[:], me.gates[F_ROW:F_ROW + NH], gate_b[F_ROW:F_ROW + NH], 0.0, ALU.add, ALU.min))
                me.link(dve.tensor_tensor(fg[:], fg[:], ltmp, ALU.subtract))
                for b in range(PB):
                    w = slice(b * S, (b + 1) * S)
                    ins = dve.tensor_tensor_scan(cs[:, w], ones_row[:], fg[:, w], 0.0, ALU.mult, ALU.add)
                me.link(ins)

            def scan(p):
                wait(dve, dec_ready, 8 * p)
                me.link(dve.scalar_tensor_tensor(out=g_rows[0:NH], in0=me.gates[0:NH], scalar=gate_b[0:NH], in1=cs[:], op0=ALU.add, op1=ALU.subtract))
                for b in range(PB):
                    w = slice(b * S, (b + 1) * S)
                    ins = dve.tensor_tensor_scan(g_max[:, w], g_rows[0:NH, w], g_rows[0:NH, w], -3.0e38, ALU.max, ALU.max)
                me.link(ins)
                me.link(dve.tensor_copy(g_part[0:NH], g_max[:]))
                dve.tensor_tensor(g_part[F_ROW:F_ROW + NH], g_max[:], g_part[0:NH].bitcast(F32), ALU.subtract)
                dve.tensor_tensor(g_rows[F_ROW:F_ROW + NH], cs[:], g_max[:], ALU.add).then_inc(rows_ready, 1)

            def sx(p, b, h):
                me.bank_filled()
                dve.wait_ge(dec_ready, 8 * p + 4 * b + h + 1)
                wait(dve, u_ready, 8 * p + 4 * b + h - 3)
                dve.scalar_tensor_tensor(out=cmat[:, h].rearrange("p a b -> p (a b)"), in0=me.bank[:, 0:3 * P], scalar=QK_SCALE,
                                         in1=dec[:, h].rearrange("p a b -> p (a b)"), op0=ALU.mult, op1=ALU.mult).then_inc(c_ready, 1)

            def ustat_step(p, b, h):
                dve.wait_ge(u_ready, 8 * p + 4 * b + h + 1)
                for t in range(T):
                    ins = dve.bn_stats(ustat[:, b * T * NH + t * NH + h], um[:, b * T + t, h, 0:DH])
                if h == NH - 1:
                    me.link(ins)

            def tail_a(p, b):
                n = T * NH
                s = um[:, b * T:(b + 1) * T, :, DH:DH + 1].rearrange("p t h o -> p (t h o)")
                un, ut = unorm[:, b], utmp[:, b]
                me.link(dve.tensor_copy(ut, s))
                me.link(dve.scalar_tensor_tensor(out=un, in0=ut, scalar=-1.0, in1=ut, op0=ALU.mult, op1=ALU.max))
                dve.wait_ge(cols_ready, 2 * p + b + 1)
                me.link(dve.tensor_tensor(un, un, e_col[:, b * T:(b + 1) * T].rearrange("p t h -> p (t h)"), ALU.max))
                me.link(dve.tensor_scalar(un, un, EPS_GATE, None, ALU.add))
                me.link(dve.scalar_tensor_tensor(out=ut, in0=un, scalar=EPS_HEAD, in1=un, op0=ALU.mult, op1=ALU.mult), alone=True)
                for k in range(n):
                    ins = dve.bn_aggr(umv[:, b * n + k], ustat[:, b * n + k])
                me.link(ins)
                dve.tensor_tensor(uvar[:, b], ut, umv[:, b * n:(b + 1) * n, 1], ALU.add).then_inc(u_var, 1)

            def norm(p, b, t):
                n = T * NH
                if t == 0:
                    dve.wait_ge(u_rstd, 2 * p + b + 1)
                    wait(dve, x12_ready, 2 * p - 1 + b)
                for h in range(NH):
                    k = t * NH + h
                    ins = dve.tensor_scalar(x1[:, b * T + t, h * DH:(h + 1) * DH], um[:, b * T + t, h, 0:DH],
                                            umv[:, b * n + k, 0:1], urstd[:, b, k:k + 1], ALU.subtract, ALU.mult)
                me.link(ins)

            def res(p, b, t):
                g = b * T + t
                me.link(dve.tensor_tensor(x1[:, g], x1[:, g], on_row[:], ALU.mult))
                dve.wait_ge(xres_loaded, 16 * p + 16)
                me.link(dve.tensor_tensor(x1[:, g], x1[:, g], x_res[:, g], ALU.add))

            def tail_b(p, b):
                for g in (b * T, b * T + 1):
                    ins = dve.bn_stats(stat1[:, g], x1[:, g])
                me.link(ins, alone=True)
                for g in (b * T, b * T + 1):
                    ins = dve.bn_aggr(mv1[:, g], stat1[:, g])
                ins.then_inc(x1_ready, 1)

            def tail_c(p, b):
                dve.wait_ge(x1_rstd, 2 * p + b + 1)
                wait(dve, n_ready, 2 * p)
                for g in (b * T, b * T + 1):
                    ins = dve.tensor_scalar(xn[:, g], x1[:, g], mv1[:, g, 0:1], r2[:, g:g + 1], ALU.subtract, ALU.mult)
                ins.then_inc(xn_ready, 1)

            def s_step(p, b, s):
                me.bank_filled()
                dve.tensor_reduce(neg_max[:, b, s], me.bank[:].rearrange("p (u k) -> p u k", u=2), AX.X, ALU.max,
                                  negate=True).then_inc(max_ready, 1)

            def pn(p, b, s):
                dve.wait_ge(exp_done, 8 * p + 4 * b + s + 1)
                dve.reciprocal(p_inv[:, b, s], p_sum[:, b, s]).then_inc(inv_ready, 1)

            def o(p, k):
                me.bank_filled()
                if k == 0:
                    dve.wait_ge(x12_ready, 2 * p + 2)
                for b in range(PB):
                    dst = x12[k * TE:(k + 1) * TE, b * T, 0:D >> k]
                    ins = dve.tensor_tensor(dst, dst, me.bank[b * TE:(b + 1) * TE, 0:D >> k], ALU.add)
                if k == 1:
                    for e in range(2):
                        w = P >> e
                        dst = x12[e * TE:(e + 1) * TE, 1:PB * T:T, 0:w]
                        ins = dve.tensor_tensor(dst, dst, me.bank[e * TE:(e + 1) * TE, S:S + PB * P].rearrange("p (b n) -> p b n", b=PB)[:, :, 0:w], ALU.add)
                ins.then_inc(o_added, 1)

            me.walk(dict(xs=xs, gsum=gsum, scan_f=scan_f, scan=scan, sx=sx, ustat=ustat_step, tail_a=tail_a, norm=norm, res=res, tail_b=tail_b, tail_c=tail_c,
                         s=s_step, pn=pn, o=o))

        @block.scalar
        def _(act):
            me = Engine(act, "scalar")

            def copy(dst, src):
                return act.activation(dst, src, ACT.Copy)

            def add(dst, src, bias, scale=1.0):
                return act.activation(dst, src, ACT.Identity, bias=bias, scale=scale)

            def xt(p, b, cc):
                me.bank_filled()
                wait(act, c_ready, 8 * p)
                copy(xq_t[:, 2 * cc:2 * cc + 2, b], me.bank[:].rearrange("p (c i) -> p c i", c=2)).then_inc(xqt_ready, 1)

            def gsum(p):
                me.bank_filled()
                me.link(act.activation(ltmp, me.bank[F_ROW:F_ROW + NH], ACT.Abs, bias=gate_b[F_ROW:F_ROW + NH]))

            def lsg(p):
                me.link(act.activation(ltmp, ltmp, ACT.Exp, scale=-1.0))
                act.activation(ltmp, ltmp, ACT.Ln, bias=1.0).then_inc(ln_ready, 1)

            def cols(p, b):
                me.bank_filled()
                wait(act, x1_ready, 2 * p - 1 + b)
                g = slice(b * T, (b + 1) * T)
                v = me.bank[:, 0:T * P].rearrange("p (t r) -> p t r", t=T)
                copy(g_col[:, g], v[:, :, 0:NH])
                act.activation(e_col[:, g], v[:, :, F_ROW:F_ROW + NH], ACT.Exp, scale=-1.0).then_inc(cols_ready, 1)

            def marg(p, b, h):
                me.bank_filled()
                act.wait_ge(cols_ready, 2 * p + b + 1)
                wait(act, c_ready, 8 * p + 4 * b + h - 3)
                v = me.bank[:, 0:3 * P].rearrange("p (n q) -> p n q", n=3)
                act.activation(dec[:, h, 0:3:2], v[:, 0:3:2], ACT.Exp, bias=g_col[:, b * T, h:h + 1])
                act.activation(dec[:, h, 1], v[:, 1], ACT.Exp, bias=g_col[:, b * T + 1, h:h + 1]).then_inc(dec_ready, 1)

            def u(p, b, h):
                me.bank_filled()
                if h == 0:
                    wait(act, x1_ready, 2 * p - 1 + b)
                v = me.bank[:].rearrange("p (t n) -> p t n", t=T)[:, :, 0:DH + 1]
                copy(um[:, b * T:(b + 1) * T, h], v).then_inc(u_ready, 1)

            def nt(p, k):
                me.bank_filled()
                wait(act, v_ready, 4 * p)
                if k == 0:
                    v = me.bank[:].rearrange("p (b i) -> p b i", b=PB)
                    add(n0[0:TE], v[0:TE], nb[0:TE, 0:1], nw[0:TE, 0:1])
                    add(n0[TE:P, :, 0:3 * TE], v[TE:P, :, 0:3 * TE], nb[TE:P, 0:1], nw[TE:P, 0:1]).then_inc(n_ready, 1)
                else:
                    add(n1[:].rearrange("p b i -> p (b i)"), me.bank[:, 0:S], nb[:, 1:2], nw[:, 1:2])
                    for c in range(2):
                        ins = add(n2[:, c].rearrange("p b i -> p (b i)"), me.bank[:, S + c * P:S + (c + 1) * P], nb[:, 2 + c:3 + c], nw[:, 2 + c:3 + c])
                    ins.then_inc(n_ready, 1)

            def k_step(p, c):
                me.bank_filled()
                add(kt[:, c].rearrange("p b i -> p (b i)"), me.bank[:], kb[:, c:c + 1]).then_inc(k_ready, 1)

            def q0_step(p):
                me.bank_filled()
                for k in range(2):
                    rows = slice(k * FH, (k + 1) * FH)
                    ins = add(q0[rows, k].rearrange("p b i -> p (b i)"), me.bank[rows], qb_s[rows, 0:1], ATT_SCALE)
                ins.then_inc(q_ready, 1)

            def q1_step(p):
                me.bank_filled()
                for k in range(2):
                    rows = slice(k * FH, (k + 1) * FH)
                    add(q1[rows, k].rearrange("p b i -> p (b i)"), me.bank[rows, 0:S], qb_s[rows, 1:2], ATT_SCALE)
                for c in range(2):
                    v = me.bank[:, S + c * P:S + (c + 1) * P].rearrange("p (b i) -> p b i", b=PB)
                    for k in range(2):
                        rows = slice(k * FH, (k + 1) * FH)
                        ins = add(q23[rows, c, :, k], v[rows], qb_s[rows, 2 + c:3 + c], ATT_SCALE)
                ins.then_inc(q_ready, 1)

            def v_step(p, k):
                me.bank_filled()
                if k < 2:
                    ins = copy(vf[:, k * T + 1], me.bank[:])
                else:
                    for b in range(PB):
                        ins = copy(vf[(k - 2) * TE:(k - 1) * TE, b * T], me.bank[b * TE:(b + 1) * TE])
                ins.then_inc(v_ready, 1)

            def gate(p):
                me.bank_filled()
                wait(act, rows_ready, p)
                copy(gate_part[:], me.bank[:]).then_inc(gpart_ready, 1)

            def s_step(p, b, s):
                act.wait_ge(max_ready, 8 * p + 4 * b + s + 1)
                for k in range(2):
                    ins = act.activation(prob[:, b, s, k], me.bank[:, k * S:(k + 1) * S], ACT.Exp, bias=neg_max[:, b, s, k:k + 1],
                                         accum_out=p_sum[:, b, s, k:k + 1])
                ins.then_inc(exp_done, 1)

            def pt(p, b, s):
                me.bank_filled()
                copy(prob_t[:, b, :, s].rearrange("p k u q -> p k (u q)"), me.bank[:].rearrange("p (k n) -> p k n", k=T)).then_inc(probt_ready, 1)

            def pv0(p, b):
                me.bank_filled()
                wait(act, o_added, 2 * p)
                add(a0[:, b, 0:3 * TE], me.bank[:, 0:3 * TE], vb[:, 0:1])
                add(a0[0:TE, b, 3 * TE:S], me.bank[0:TE, 3 * TE:S], vb[0:TE, 0:1]).then_inc(a_ready, 1)

            def pv1(p, b):
                me.bank_filled()
                add(a1[:, b], me.bank[:, 0:P], vb[:, 1:2])
                for c in range(2):
                    n = P + c * TE
                    ins = add(a23[:, b, c], me.bank[:, n:n + TE], vb[:, 2 + c:3 + c])
                ins.then_inc(a_ready, 1)

            act.wait_ge(consts_in, N_CONST)
            act.wait_ge(consts_ready, 2)
            act.wait_ge(zeros_made, 2)
            me.walk(dict(xt=xt, gate=gate, gsum=gsum, lsg=lsg, cols=cols, marg=marg, u=u, nt=nt, k=k_step, q0=q0_step, q1=q1_step, v=v_step,
                         s=s_step, pt=pt, pv0=pv0, pv1=pv1))

        @block.tensor
        def _(pe):
            me = Engine(pe, "tensor")

            def mm(dst, lhs, rhs, first, last):
                return pe.matmul(dst, lhs, rhs, start=first, stop=last)

            def xt(p, b, cc):
                me.bank_free()
                pe.wait_ge(xq_ready, 2 * p + b + 1)
                for c in range(2):
                    for t in range(T):
                        n = (c * T + t) * P
                        f = (2 * cc + c) * P
                        ins = pe.transpose(me.bank[:, n:n + P], x_in[:, b * T + t, f:f + P], ident[:])
                ins.then_inc(me.ring.filled, 1)

            def gate(p):
                me.bank_free()
                pe.wait_ge(xqt_ready, 4 * p + 4)
                pe.wait_ge(kx_loaded, 16 * p + 16)
                for c in range(C):
                    mm(me.bank[c * GT:(c + 1) * GT], gate_w[:, c], xq_t[:, c].rearrange("p b i -> p (b i)"), True, False)
                for c in range(C):
                    dst = me.bank[c * GT:(c + 1) * GT].rearrange("p (b i) -> p b i", b=PB)
                    ins = mm(dst, gate_w[:, C + c], kx_t[:, c:PB * C:C], False, True)
                ins.then_inc(me.ring.filled, 1)

            def gsum(p):
                me.bank_free()
                pe.wait_ge(gpart_ready, p + 1)
                mm(me.bank[0:F_ROW + NH], gate_sel[:], gate_part[:], True, True).then_inc(me.ring.filled, 1)

            def cols(p, b):
                me.bank_free()
                pe.wait_ge(rows_ready, p + 1)
                for t in range(T):
                    w = slice((b * T + t) * P, (b * T + t + 1) * P)
                    ins = pe.transpose(me.bank[:, t * P:(t + 1) * P], g_rows[:, w], ident[:])
                ins.then_inc(me.ring.filled, 1)

            def marg(p, b, h):
                me.bank_free()
                pe.wait_ge(rows_ready, p + 1)
                mm(me.bank[:, 0:S], neg_sel[:, h], g_part[:, b * S:(b + 1) * S], True, False)
                mm(me.bank[:, 0:S], ident_r[:], mask[:].rearrange("p n q -> p (n q)"), False, True)
                mm(me.bank[:, S:S + P], neg_sel[:, h], g_part[:, b * S + P:(b + 1) * S], True, True).then_inc(me.ring.filled, 1)

            def sx(p, b, h):
                me.bank_free()
                k = kx_t[:, b * C + h]
                mm(me.bank[:, 0:4 * P].rearrange("p (n i) -> p n i", n=2)[:, :, 0:P], k[:, 0:P], xq_t[:, h, b].rearrange("p (t i) -> p t i", t=T), True, True)
                mm(me.bank[:, P:2 * P], k[:, P:S], xq_t[:, h, b, P:S], True, True).then_inc(me.ring.filled, 1)

            def u(p, b, h):
                me.bank_free()
                pe.wait_ge(c_ready, 8 * p + 4 * b + h + 1)
                pe.wait_ge(vx_loaded, 64 * p + 64)
                v0, v1 = vx[:, b * T, h], vx[:, b * T + 1, h]
                mm(me.bank[:, 0:DH + 1], cmat[:, h, 0], v0, True, True)
                mm(me.bank[:, S:S + DH + 1], cmat[:, h, 2], v0, True, False)
                mm(me.bank[:, S:S + DH + 1], cmat[:, h, 1], v1, False, True).then_inc(me.ring.filled, 1)

            def nt(p, k):
                me.bank_free()
                pe.wait_ge(xn_ready, 2 * p + 2)
                for b in range(PB):
                    if k == 0:
                        for t in range(T):
                            n = (b * T + t) * P
                            ins = pe.transpose(me.bank[:, n:n + P], xn[:, b * T + t, 0:P], ident[:])
                    else:
                        ins = pe.transpose(me.bank[:, b * P:(b + 1) * P], xn[:, b * T, P:2 * P], ident[:])
                        for c in range(2):
                            n = S + c * P + b * TE
                            ins = pe.transpose(me.bank[:, n:n + TE], xn[0:TE, b * T, (2 + c) * P:(3 + c) * P], ident[0:TE, 0:TE])
                ins.then_inc(me.ring.filled, 1)

            def project(dst, w, c, tokens):
                cols = slice(c * P, (c + 1) * P)
                inputs = [n0, n1, n2[:, 0], n2[:, 1]]
                for k in reversed(range(C)):
                    seen = min(tokens, (S, 2 * TE, TE, TE)[k])
                    src = inputs[k][:, :, 0:seen]
                    ins = pe.matmul(dst[:, :, 0:seen], w[:, k, cols], src, start=k == C - 1, stop=k == 0, skip_group_check=True)
                return ins

            def weights_loaded(p):
                if isinstance(p, int) and p == 0:
                    pe.wait_ge(weights_in, 64)

            def k_step(p, c):
                me.bank_free()
                pe.wait_ge(n_ready, 2 * p + 2)
                weights_loaded(p)
                project(me.bank[:].rearrange("p (b i) -> p b i", b=PB), wk, c, S).then_inc(me.ring.filled, 1)

            def q0_step(p):
                me.bank_free()
                pe.wait_ge(n_ready, 2 * p + 2)
                weights_loaded(p)
                project(me.bank[:].rearrange("p (b i) -> p b i", b=PB), wq, 0, S).then_inc(me.ring.filled, 1)

            def q1_step(p):
                me.bank_free()
                pe.wait_ge(n_ready, 2 * p + 2)
                weights_loaded(p)
                project(me.bank[:, 0:S].rearrange("p (b i) -> p b i", b=PB), wq, 1, 2 * TE)
                for c in range(2):
                    ins = project(me.bank[:, S + c * P:S + (c + 1) * P].rearrange("p (b i) -> p b i", b=PB), wq, 2 + c, TE)
                ins.then_inc(me.ring.filled, 1)

            def pair_of_batches(dst, inputs, w, n):
                for c, tokens in enumerate(inputs):
                    for b in range(PB):
                        ins = mm(dst[b * TE:(b + 1) * TE], tokens[:, b], w[:, c, 0:n], c == 0, c == len(inputs) - 1)
                return ins

            def v_step(p, k):
                me.bank_free()
                pe.wait_ge(n_ready, 2 * p + (1 if k < 2 else 2))
                weights_loaded(p)
                if k < 2:
                    ins = mm(me.bank[:], n0[:, k, P:S], wv[:, 0], True, True)
                else:
                    w = slice((k - 2) * TE, (k - 1) * TE)
                    tokens = [n0[:, :, w], n1[:, :, w], n2[:, 0], n2[:, 1]][0:C >> (k - 2)]
                    ins = pair_of_batches(me.bank[:], tokens, wv, D)
                ins.then_inc(me.ring.filled, 1)

            def s_step(p, b, s):
                me.bank_free()
                pe.wait_ge(q_ready, 2 * p + 2)
                pe.wait_ge(k_ready, 4 * p + 4)
                for u in range(2):
                    dst = me.bank[:, u * S:(u + 1) * S]
                    if s < 2:
                        ins = mm(dst, q0[:, u, b, s * P:(s + 1) * P], kt[:, 0, b], True, True)
                    elif s == 2:
                        ins = mm(dst, q1[:, u, b], kt[:, 1, b], True, True)
                    else:
                        ins = mm(dst, q23[:, u, b].rearrange("p k i -> p (k i)"), kt[:, 2 + u, b], True, True)
                ins.then_inc(me.ring.filled, 1)

            def pt(p, b, s):
                me.bank_free()
                pe.wait_ge(prob_ready, 8 * p + 4 * b + s + 1)
                for k in range(T):
                    for u in range(2):
                        n = (k * 2 + u) * P
                        ins = pe.transpose(me.bank[:, n:n + P], prob[:, b, s, u, k * P:(k + 1) * P], ident[:])
                ins.then_inc(me.ring.filled, 1)

            def pair_of_heads(dst, b, c, probs):
                for k in range(T):
                    for u in range(2):
                        f = c * P + u * FH
                        ins = mm(dst[u * FH:(u + 1) * FH], vf[:, b * T + k, f:f + FH], probs(k, u), k == 0, k == T - 1)
                return ins

            def pv0(p, b):
                me.bank_free()
                pe.wait_ge(probt_ready, 8 * p + 4 * b + 2)
                pe.wait_ge(v_ready, 4 * p + 4)
                pair_of_heads(me.bank[:, 0:S].rearrange("p (s q) -> p s q", s=2), b, 0,
                              lambda k, u: prob_t[:, b, k, 0:2, u]).then_inc(me.ring.filled, 1)

            def pv1(p, b):
                me.bank_free()
                pe.wait_ge(probt_ready, 8 * p + 4 * b + 4)
                pair_of_heads(me.bank[:, 0:P], b, 1, lambda k, u: prob_t[:, b, k, 2, u])
                for c in range(2):
                    n = P + c * TE
                    ins = pair_of_heads(me.bank[:, n:n + TE], b, 2 + c, lambda k, u: prob_t[:, b, k, 3, c, u * TE:(u + 1) * TE])
                ins.then_inc(me.ring.filled, 1)

            def o(p, k):
                me.bank_free()
                pe.wait_ge(a_ready, 4 * p + 4)
                w = slice(k * TE, (k + 1) * TE)
                inputs = [a0[:, :, w], a1[:, :, w], a23[:, :, 0], a23[:, :, 1]][0:C >> k]
                ins = pair_of_batches(me.bank[:, 0:D >> k], inputs, wo, D >> k)
                if k == 1:
                    for b in range(PB):
                        ins = mm(me.bank[:, S + b * P:S + (b + 1) * P], a0[:, b, P:S], wo[:, 0, 0:P], True, True)
                ins.then_inc(me.ring.filled, 1)

            pe.wait_ge(ident_made, 17)
            pe.wait_ge(zeros_made, 2)
            pe.wait_ge(consts_ready, 2)
            me.walk(dict(xt=xt, gate=gate, gsum=gsum, cols=cols, marg=marg, sx=sx, u=u, nt=nt, k=k_step, q0=q0_step, q1=q1_step, v=v_step,
                         s=s_step, pt=pt, pv0=pv0, pv1=pv1, o=o))


_OUT = ((B, S, D), "float32")


def kernel(**inputs):
    import numpy as np
    import concourse.bacc as bacc
    from concourse.bass_utils import run_bass_kernel_spmd as run

    def get(name):
        return np.asarray(inputs[name])

    def column(name):
        return get(name).reshape(C, P).T

    laid = {
        "x": get("x"), "ctx": get("ctx_1024"), "ctx_t": get("ctx_1024").transpose(0, 2, 1),
        "ig_w": get("L0_xattn_igate_kernel"), "ig_b": get("L0_xattn_igate_bias").reshape(NH, 1),
        "fg_w": get("L0_xattn_fgate_kernel"), "fg_b": get("L0_xattn_fgate_bias").reshape(NH, 1),
        "on_scale": get("L0_xattn_outnorm_scale").reshape(1, D),
        "n_w": column("L0_ffn_norm_w"), "n_b": column("L0_ffn_norm_b"),
        "wq_t": get("L0_ffn_q_w").T, "q_b": column("L0_ffn_q_b"), "wk_t": get("L0_ffn_k_w").T, "k_b": column("L0_ffn_k_b"),
        "wv_t": get("L0_ffn_v_w").T, "v_b": column("L0_ffn_v_b"), "wo_t": get("L0_ffn_o_w").T,
        "o_b": get("L0_ffn_o_b").reshape(1, D),
    }
    nc = bacc.Bacc("TRN2", target_bir_lowering=False, num_devices=1)
    arrays, args = {}, []
    for name, a in laid.items():
        arrays[f"in_{name}"] = np.ascontiguousarray(a)
        args.append(nc.dram_tensor(f"in_{name}", a.shape, mybir.dt.from_np(a.dtype), kind="ExternalInput").ap())
    args.append(nc.dram_tensor("out_0", _OUT[0], F32, kind="ExternalOutput").ap())
    xattn_ffn(nc, *args)
    r = run(nc, [arrays], core_ids=[0])
    return r.results[0]["out_0"]
```
